# Optimizing a Trainium2 kernel written in Bass

```python
import numpy as np
import jax
import jax.numpy as jnp

def _softmax(x, axis=-1):
    return jax.nn.softmax(x, axis=axis)

def _gelu(x):
    return jax.nn.gelu(x, approximate=True)

def _silu(x):
    return jax.nn.silu(x)

def _sigmoid(x):
    return jax.nn.sigmoid(x)

def _layernorm(x, axis=-1, eps=1e-05):
    m = jnp.mean(x, axis=axis, keepdims=True)
    v = jnp.var(x, axis=axis, keepdims=True)
    return (x - m) / jnp.sqrt(v + eps)

def _scatter_add(tgt, idx, src, axis=0):
    return tgt.at[idx].add(src)

def _segment_sum(src, seg, n):
    return jax.ops.segment_sum(src, seg, n)
kernel_name = 'mk_seq_postln_d1_jaxref_r4_f06ab0'

def setup_inputs(seed: int=0):
    np.random.seed(seed)
    _w = jnp.asarray

    def _L0_attn_setup():
        import jax, jax.numpy as jnp
        import numpy as np
        D_MODEL = 256
        D_STATE = 128
        BATCH = 16
        SEQ = 512
        LN_EPS = 1e-05
        key = jax.random.key(seed)
        ks = jax.random.split(key, 4)
        x = jax.random.normal(ks[0], (BATCH, SEQ, D_MODEL), dtype=jnp.float32)
        A = jax.random.normal(ks[1], (D_STATE, D_STATE), dtype=jnp.float32) * 0.01
        B = jax.random.normal(ks[2], (D_STATE, D_MODEL), dtype=jnp.float32) * 0.01
        C = jax.random.normal(ks[3], (D_MODEL, D_STATE), dtype=jnp.float32) * 0.01
        D = jnp.ones((D_MODEL,), dtype=jnp.float32)
        gamma = jnp.ones((D_MODEL,), dtype=jnp.float32)
        beta = jnp.zeros((D_MODEL,), dtype=jnp.float32)
        return {'x': x, 'A': A, 'B': B, 'C': C, 'D': D, 'gamma': gamma, 'beta': beta}
    _L0_attn_in = _L0_attn_setup()

    def _L0_ffn_setup():
        import jax, jax.numpy as jnp
        import numpy as np
        B, S, H = (2, 1024, 256)
        I = 128
        E = 8
        TOPK = 2
        NGROUP = 2
        TOPK_GROUP = 1
        ROUTED_SCALE = 1.0

        def _silu(x):
            return x * jax.nn.sigmoid(x)
        key = jax.random.key(seed)
        ks = jax.random.split(key, 9)

        def w(k, shape, s=0.05):
            return jax.random.normal(k, shape, dtype=jnp.float32) * s
        return {'hidden_states': jax.random.normal(ks[0], (B, S, H), dtype=jnp.float32), 'router_weight': w(ks[1], (E, H)), 'correction_bias': w(ks[2], (E,)), 'w_gate': w(ks[3], (E, H, I)), 'w_up': w(ks[4], (E, H, I)), 'w_down': w(ks[5], (E, I, H)), 'sw_gate': w(ks[6], (H, I)), 'sw_up': w(ks[7], (H, I)), 'sw_down': w(ks[8], (I, H))}
    _L0_ffn_in = _L0_ffn_setup()
    _d = {'L0_attn_x': _L0_attn_in['x'], 'L0_attn_A': _L0_attn_in['A'], 'L0_attn_B': _L0_attn_in['B'], 'L0_attn_C': _L0_attn_in['C'], 'L0_attn_D': _L0_attn_in['D'], 'L0_attn_gamma': _L0_attn_in['gamma'], 'L0_attn_beta': _L0_attn_in['beta'], 'L0_ffn_router_weight': _L0_ffn_in['router_weight'], 'L0_ffn_correction_bias': _L0_ffn_in['correction_bias'], 'L0_ffn_w_gate': _L0_ffn_in['w_gate'], 'L0_ffn_w_up': _L0_ffn_in['w_up'], 'L0_ffn_w_down': _L0_ffn_in['w_down'], 'L0_ffn_sw_gate': _L0_ffn_in['sw_gate'], 'L0_ffn_sw_up': _L0_ffn_in['sw_up'], 'L0_ffn_sw_down': _L0_ffn_in['sw_down']}
    _x0 = _d['L0_attn_x']
    _d['L0_attn_x'] = jax.random.normal(jax.random.fold_in(jax.random.key(seed), 1), (2, 2048, 256), dtype=_x0.dtype)
    del _x0
    return _d

def reference(L0_attn_x, L0_attn_A, L0_attn_B, L0_attn_C, L0_attn_D, L0_attn_gamma, L0_attn_beta, L0_ffn_router_weight, L0_ffn_correction_bias, L0_ffn_w_gate, L0_ffn_w_up, L0_ffn_w_down, L0_ffn_sw_gate, L0_ffn_sw_up, L0_ffn_sw_down):

    def _L0_attn_ref(x, A, B, C, D, gamma, beta):
        import jax, jax.numpy as jnp
        import numpy as np
        D_MODEL = 256
        D_STATE = 128
        BATCH = 16
        SEQ = 512
        LN_EPS = 1e-05
        bsz, seq, dm = x.shape
        xB = jnp.einsum('bsd,nd->bsn', x, B)

        def step(state, xb_t):
            state = jnp.tanh(state @ A.T + xb_t)
            return (state, state)
        init = jnp.zeros((bsz, A.shape[0]), dtype=x.dtype)
        _, states = jax.lax.scan(step, init, jnp.swapaxes(xB, 0, 1))
        states = jnp.swapaxes(states, 0, 1)
        out = jnp.einsum('bsn,dn->bsd', states, C) + D * x
        y = out + x
        mu = jnp.mean(y, axis=-1, keepdims=True)
        var = jnp.mean(jnp.square(y - mu), axis=-1, keepdims=True)
        return (y - mu) * jax.lax.rsqrt(var + LN_EPS) * gamma + beta

    def _L0_ffn_ref(hidden_states, router_weight, correction_bias, w_gate, w_up, w_down, sw_gate, sw_up, sw_down):
        import jax, jax.numpy as jnp
        import numpy as np
        B, S, H = (2, 1024, 256)
        I = 128
        E = 8
        TOPK = 2
        NGROUP = 2
        TOPK_GROUP = 1
        ROUTED_SCALE = 1.0

        def _silu(x):
            return x * jax.nn.sigmoid(x)
        b, s, h = hidden_states.shape
        x = hidden_states.reshape(-1, h)
        logits = x @ router_weight.T
        scores = jax.nn.sigmoid(logits)
        scores_for_choice = scores + correction_bias[None, :]
        e_per_g = E // NGROUP
        group_scores = jax.lax.top_k(scores_for_choice.reshape(-1, NGROUP, e_per_g), 2)[0].sum(-1)
        group_idx = jax.lax.top_k(group_scores, TOPK_GROUP)[1]
        group_mask = jax.nn.one_hot(group_idx, NGROUP, dtype=scores.dtype).sum(1)
        score_mask = jnp.repeat(group_mask, e_per_g, axis=1)
        masked = jnp.where(score_mask > 0, scores_for_choice, 0.0)
        topk_idx = jax.lax.top_k(masked, TOPK)[1]
        topk_w = jnp.take_along_axis(scores, topk_idx, axis=1)
        topk_w = topk_w / (topk_w.sum(-1, keepdims=True) + 1e-20)
        topk_w = topk_w * ROUTED_SCALE
        comb = (jax.nn.one_hot(topk_idx, E, dtype=x.dtype) * topk_w[..., None]).sum(1)
        g = jnp.einsum('th,ehi->tei', x, w_gate)
        u = jnp.einsum('th,ehi->tei', x, w_up)
        y = jnp.einsum('tei,eih->teh', _silu(g) * u, w_down)
        routed = jnp.einsum('teh,te->th', y, comb).reshape(b, s, h)
        shared = _silu(hidden_states @ sw_gate) * (hidden_states @ sw_up) @ sw_down
        return routed + shared
    x = L0_attn_x
    x = _layernorm(x + _L0_attn_ref(x, L0_attn_A, L0_attn_B, L0_attn_C, L0_attn_D, L0_attn_gamma, L0_attn_beta), axis=-1)
    x = _layernorm(x + _L0_ffn_ref(x, L0_ffn_router_weight, L0_ffn_correction_bias, L0_ffn_w_gate, L0_ffn_w_up, L0_ffn_w_down, L0_ffn_sw_gate, L0_ffn_sw_up, L0_ffn_sw_down), axis=-1)
    return x

_drawn_inputs = setup_inputs


def setup_inputs(seed=0):
    import zlib

    import numpy as np

    out = dict(_drawn_inputs(seed))
    spreads = {'L0_attn_D': (1.0, 0.2), 'L0_attn_gamma': (1.0, 0.2), 'L0_attn_beta': (0.0, 0.1)}
    factors = {'L0_attn_A': 8.0, 'L0_attn_B': 6.224, 'L0_attn_C': 5.965}
    for name, (base, spread) in spreads.items():
        noise = np.random.default_rng([zlib.crc32(name.encode()), seed]).standard_normal(out[name].shape)
        drawn = base * np.exp(spread * noise) if base else spread * noise
        out[name] = jnp.asarray(drawn.astype(out[name].dtype))
    for name, factor in factors.items():
        out[name] = (out[name] * factor).astype(out[name].dtype)
    return out
```

```python
from contextlib import ExitStack

import concourse.bass as bass
from concourse import mybir

ALU = mybir.AluOpType
ACT = mybir.ActivationFunctionType
F32 = mybir.dt.float32
F16 = mybir.dt.float16
I32 = mybir.dt.int32
AX_X = mybir.AxisListType.X
RMAX = bass.bass_isa.ReduceOp.max
P = 128

LN_EPS = 1e-5
MET = 2.0 ** -20


def ssm_moe_kernel(nc, x, A, B, C, D, gamma, beta, router_weight, correction_bias,
                   w_gate, w_up, w_down, sw_gate, sw_up, sw_down, out):
    NB, S, DM = x.shape
    NS = A.shape[0]
    E, _, I = w_gate.shape
    KT = DM // P
    L = NB * S // P
    NCH = P // NB
    WARM = 4
    T4 = 4
    G = L // T4
    GT = T4 * P
    E1 = E + 1
    EPG = E // 2
    assert NS == P and I == P and DM == 2 * P and L % (2 * T4) == 0

    XS = 2.0 ** 11
    WTOP = 14
    CS = 2.0 ** 14

    with ExitStack() as ctx:
        def sb(name, shape, dt=F32):
            return ctx.enter_context(nc.sbuf_tensor(name, shape, dt))

        def sem(name):
            return ctx.enter_context(nc.semaphore(name))

        xres = sb("xres", [P, L, DM])
        xskip = sb("xskip", [P, L, DM])
        xT = sb("xT", [P, KT, L, P])
        states = sb("states", [P, L, P])
        run_state = sb("run_state", [P, 2, P])
        seed = sb("seed", [P, NB, NCH])
        fb_state = sb("fb_state", [P, 2, NB])
        met_diff = sb("met_diff", [P, NB, NCH - 1])
        met_row = sb("met_row", [P, 2])
        met = sb("met", [P, 1], I32)

        ident = sb("ident", [P, P])
        ident16 = sb("ident16", [P, P], F16)
        A_sb = sb("A_sb", [P, NS])
        B_sb = sb("B_sb", [P, DM])
        C_sb = sb("C_sb", [P, KT, NS])
        rw_sb = sb("rw_sb", [E, DM])
        AT = sb("AT", [P, NS])
        BT = sb("BT", [P, KT, NS])
        CT = sb("CT", [P, KT, P])
        rwT = sb("rwT", [P, KT, E])
        rw16 = sb("rw16", [P, 2, KT, E], F16)
        D_bc = sb("D_bc", [P, DM])
        gamma_bc = sb("gamma_bc", [P, DM])
        beta_bc = sb("beta_bc", [P, DM])
        cbias_bc = sb("cbias_bc", [P, E])

        wg = sb("wg", [P, E1, KT, I])
        wu = sb("wu", [P, E1, KT, I])
        wd = sb("wd", [P, E1, DM])
        wg16 = sb("wg16", [P, 2, E1, KT, I], F16)
        wu16 = sb("wu16", [P, 2, E1, KT, I], F16)
        wd16 = sb("wd16", [P, 2, E1, DM], F16)
        wmax = sb("wmax", [P, 4])
        wmax_all = sb("wmax_all", [P, 4])
        wpow = sb("wpow", [P, 4])
        wscale = sb("wscale", [P, 4])
        g_un = sb("g_un", [P, 1])
        u_un = sb("u_un", [P, 2])
        l_un = sb("l_un", [P, 1])
        y_un = sb("y_un", [P, 2])

        late = xT[:, :, :, :].rearrange("p k l c -> p (k l c)")
        y1 = late[:, 0:T4 * DM].rearrange("p (t d) -> p t d", t=T4)
        x2 = late[:, T4 * DM:3 * T4 * DM].rearrange("p (a t d) -> p a t d", a=2, t=T4)
        sg, gu, h = (late[:, 3 * T4 * DM + i * 2 * GT:3 * T4 * DM + (i + 1) * 2 * GT].rearrange("p (b t) -> p b t", b=2)
                     for i in range(3))
        gstates = late[:, 3 * T4 * DM + 6 * GT:3 * T4 * DM + 7 * GT].rearrange("p (t c) -> p t c", t=T4)
        st = sb("st", [P, 3, T4, 6])
        mv = sb("mv", [P, 3, T4, 2])
        rstd = sb("rstd", [P, 3, 2, T4])
        neghalf = sb("neghalf", [P, T4])
        carrier = sb("carrier", [P, 1])
        eps = sb("eps", [P, T4])
        x2T = sb("x2T", [P, 2, 2, KT, GT], F16)
        th = sb("th", [P, T4, E])
        score = sb("score", [P, T4, E])
        choice = sb("choice", [P, T4, E])
        more, less = sb("more", [P, T4, E // 2]), sb("less", [P, T4, E // 2])
        top, second, other, mask = (sb(n, [P, T4, 2]) for n in ("top", "second", "other", "mask"))
        pick1, pick2, peak = sb("pick1", [P, T4, E]), sb("pick2", [P, T4, E]), sb("peak", [P, T4, 2])
        countdown = sb("countdown", [P, T4, E])
        h16 = sb("h16", [P, 3, 2, GT], F16)
        comb = sb("comb", [P, T4, 2, E], F16)
        combT = sb("combT", [2 * E, GT], F16)
        pick = sb("pick", [2 * E, E, P], F16)

        bank = [ctx.enter_context(nc.psum_tensor(f"bank{i}", [P, 512], F32)) for i in range(8)]
        ps_scan = bank[0:2]
        ps_xT = bank[2:6]
        ps_g, ps_u, ps_y = bank[0:2], bank[2:4], bank[4:6]
        ps_comb, ps_misc = bank[6], bank[7]
        ps_misc16 = ps_misc[:, :].bitcast(F16)

        x_in = [sem(f"x_in{i}") for i in range(L // T4)]
        mats_in, vecs_in, w_in = sem("mats_in"), sem("vecs_in"), sem("w_in")
        const_step, consts = sem("const_step"), sem("consts")
        mats_turned, mats_done = sem("mats_turned"), sem("mats_done")
        xT_turned, xT_done = sem("xT_turned"), sem("xT_done")
        seed_clear, scan_mm, scan_tanh = sem("seed_clear"), sem("scan_mm"), sem("scan_tanh")
        met_step, met_part, met_all, met_known = sem("met_step"), sem("met_part"), sem("met_all"), sem("met_known")
        fb_mm, fb_tanh, fb_kept = sem("fb_mm"), sem("fb_tanh"), sem("fb_kept")
        runs_done = sem("runs_done")
        skip_done, res_done = sem("skip_done"), sem("res_done")
        wmax_part, wmax_known, wstep, weights_ready = sem("wmax_part"), sem("wmax_known"), sem("wstep"), sem("weights_ready")
        rwT_ready, rw_ready = sem("rwT_ready"), sem("rw_ready")
        gstates_ready, c_done, y1_done = sem("gstates_ready"), sem("c_done"), sem("y1_done")
        st1_done, mv1_done, scaled1, z1_done = sem("st1_done"), sem("mv1_done"), sem("scaled1"), sem("z1_done")
        st2_done, mv2_done, x2_ready = sem("st2_done"), sem("mv2_done"), sem("x2_ready")
        rstd_step, rstd1_ready, rstd2_ready, rstd3_ready = sem("rstd_step"), sem("rstd1_ready"), sem("rstd2_ready"), sem("rstd3_ready")
        x2_turned, x2_high, x2_low = sem("x2_turned"), sem("x2_high"), sem("x2_low")
        logits_done, th_done, route_step = sem("logits_done"), sem("th_done"), sem("route_step")
        comb_turned, combT_ready = sem("comb_turned"), sem("combT_ready")
        up_done, silu_done, gu_done, cb_done, h_done, h_high, h_low, down_done = (
            sem("up_done"), sem("silu_done"), sem("gu_done"), sem("cb_done"), sem("h_done"),
            sem("h_high"), sem("h_low"), sem("down_done"))
        z2_done, st3_done, mv3_done, out_ready, out_sent = (
            sem("z2_done"), sem("st3_done"), sem("mv3_done"), sem("out_ready"), sem("out_sent"))

        x_dram = x.rearrange("b s d -> (b s) d").rearrange("(p l) d -> p l d", l=L)
        out_dram = out.rearrange("b s d -> (b s) d").rearrange("(p l) d -> p l d", l=L)

        chunks = [L // T4 - 1] + list(range(L // T4 - 1))
        pairs = [c * T4 // 2 + j for c in chunks for j in range(T4 // 2)]
        ROUTED = [(w_gate, wg), (w_up, wu)]
        SHARED = [(sw_gate, wg), (sw_up, wu)]
        NMAT, NVEC, NW = 4, 4, 6
        STEPS = 27

        block = ctx.enter_context(nc.Block())

        @block.sync
        def _(sp):
            for n, c in enumerate(chunks):
                sp.dma_start(xres[:, c * T4:(c + 1) * T4, :], x_dram[:, c * T4:(c + 1) * T4, :]).then_inc(x_in[c], 16)
                if n == 0:
                    sp.dma_start(A_sb[:, :], A).then_inc(mats_in, 16)
                    sp.dma_start(B_sb[:, :], B).then_inc(mats_in, 16)
                    sp.dma_start(C_sb[:, :, :], C.rearrange("(k p) n -> p k n", p=P)).then_inc(mats_in, 16)
                    sp.dma_start(rw_sb[:, :], router_weight).then_inc(mats_in, 16)
            sp.dma_start(D_bc[:, :], D.partition_broadcast(P)).then_inc(vecs_in, 16)
            sp.dma_start(gamma_bc[:, :], gamma.partition_broadcast(P)).then_inc(vecs_in, 16)
            sp.dma_start(beta_bc[:, :], beta.partition_broadcast(P)).then_inc(vecs_in, 16)
            sp.dma_start(cbias_bc[:, :], correction_bias.partition_broadcast(P)).then_inc(vecs_in, 16)
            for dram, tile in ROUTED:
                sp.dma_start(tile[:, 1:E1, :, :].rearrange("p e k i -> p (e k) i"),
                             dram.rearrange("e (k p) i -> p (e k) i", p=P)).then_inc(w_in, 16)
            for dram, tile in SHARED:
                sp.dma_start(tile[:, 0, :, :], dram.rearrange("(k p) i -> p k i", p=P)).then_inc(w_in, 16)
            sp.dma_start(wd[:, 1:E1, :], w_down.rearrange("e i d -> i e d")).then_inc(w_in, 16)
            sp.dma_start(wd[:, 0, :], sw_down).then_inc(w_in, 16)

            def send(g):
                sp.wait_ge(out_ready, (g + 1) * T4)
                sp.dma_start(out_dram[:, bass.ds(g * T4, T4), :], xskip[:, bass.ds(g * T4, T4), :]).then_inc(out_sent, 16)

            with sp.Fori(0, G) as g:
                send(g)
            sp.wait_ge(out_sent, 16 * G)

        @block.tensor
        def _(pe):
            pe.wait_ge(consts, 2)
            pe.wait_ge(mats_in, 16 * NMAT)
            pe.transpose(ps_xT[2][:, 0:P], A_sb[:, :], ident[:, :])
            for k in range(KT):
                pe.transpose(ps_xT[2][:, (k + 1) * P:(k + 2) * P], B_sb[:, k * P:(k + 1) * P], ident[:, :])
            for k in range(KT):
                pe.transpose(ps_xT[3][:, k * P:(k + 1) * P], C_sb[:, k, :], ident[:, :])
            for k in range(KT):
                last = pe.transpose(ps_xT[3][:, KT * P + k * E:KT * P + (k + 1) * E], rw_sb[:, k * P:(k + 1) * P],
                                    ident[0:E, 0:E])
            last.then_inc(mats_turned, 1)

            def turn_x(n):
                pair = pairs[n]
                pe.wait_ge(x_in[pair * 2 // T4], 16)
                if n >= 2:
                    pe.wait_ge(xT_done, n - 1)
                for k in range(KT):
                    for j in range(2):
                        last = pe.transpose(ps_xT[n % 2][:, (k * 2 + j) * P:(k * 2 + j + 1) * P],
                                            xres[:, pair * 2 + j, k * P:(k + 1) * P], ident[:, :])
                last.then_inc(xT_turned, 1)

            def scan_step(s, tile, before):
                for k in range(KT):
                    pe.matmul(ps_scan[s % 2][:, 0:P], BT[:, k, :], xT[:, k, tile, :], start=(k == 0), stop=False)
                if s:
                    pe.wait_ge(scan_tanh, s)
                pe.matmul(ps_scan[s % 2][:, 0:P], AT[:, :], before, start=False, stop=True).then_inc(scan_mm, 1)

            pe.wait_ge(mats_done, 2)
            pe.wait_ge(seed_clear, 2)
            turn_x(0)
            turn_x(1)
            turn_x(2)
            seeds = seed[:, :, :].rearrange("p b c -> p (b c)")
            s = 0
            turned = 3
            pe.wait_ge(xT_done, 2)
            for tile in range(L - WARM, L):
                scan_step(s, tile, seeds if tile == L - WARM else run_state[:, (s - 1) % 2, :])
                s += 1
            for tile in range(L):
                if tile % 2 == 0 and turned < len(pairs):
                    turn_x(turned)
                    turned += 1
                if tile < L - WARM and tile % 2 == 0:
                    pe.wait_ge(xT_done, 3 + tile // 2)
                scan_step(s, tile, seeds if tile == 0 else run_state[:, (s - 1) % 2, :])
                s += 1
            for tile in range(L):
                scan_step(s, tile, seeds if tile == 0 else states[:, tile - 1, :])
                s += 1

            pe.wait_ge(met_known, 1)
            runs_met = pe.value_load(met[0:1, 0:1], min_val=0, max_val=1)
            with pe.If(runs_met == 0):
                with pe.Fori(0, NCH) as c:
                    with pe.Fori(0, L // 2) as l:
                        for j in range(2):
                            for k in range(KT):
                                last = pe.matmul(ps_scan[j][:, 0:NB], BT[:, k, :],
                                                 xT[:, k, l * 2 + j, :].rearrange("p (b c) -> p c b", b=NB)[:, c, :],
                                                 start=(k == 0), stop=False)
                            pe.wait_ge(fb_tanh, c * L + l * 2 + (j + 1))
                            pe.matmul(ps_scan[j][:, 0:NB], AT[:, :], fb_state[:, 1 - j, :],
                                      start=False, stop=True).then_inc(fb_mm, 1)
                pe.wait_ge(fb_kept, NCH * L)

            def piece(e, g, par):
                if e in (0, 1):
                    if e == 0:
                        if not isinstance(g, int) or g:
                            pe.wait_ge(combT_ready, g)
                    else:
                        pe.wait_ge(y1_done, g * 2 + 1)
                    pe.wait_ge(gstates_ready, g + 1)
                    for j in range(2):
                        last = pe.matmul(ps_misc[:, j * DM:(j + 1) * DM], gstates[:, 2 * e + j, :],
                                         CT[:, :, :].rearrange("p k d -> p (k d)"), start=True, stop=True)
                        last.then_inc(c_done, 1)
                elif e in (5, 6):
                    half = e - 5
                    if half == 0:
                        pe.wait_ge(x2_ready, (g + 1) * T4)
                    else:
                        pe.wait_ge(x2_low, g * 2 + 1)
                    for k in range(KT):
                        for j in range(2):
                            last = pe.transpose(ps_misc[:, (k * 2 + j) * P:(k * 2 + j + 1) * P],
                                                x2[:, par, 2 * half + j, k * P:(k + 1) * P], ident[:, :])
                    last.then_inc(x2_turned, 1)

            def logits(g, par):
                pe.wait_ge(x2_low, g * 2 + 2)
                for t in range(T4):
                    n = 0
                    for px, pw in ((0, 0), (0, 1), (1, 0)):
                        for k in range(KT):
                            last = pe.matmul(ps_misc[:, t * E:(t + 1) * E], x2T[:, par, px, k, t * P:(t + 1) * P],
                                             rw16[:, pw, k, :], start=(n == 0), stop=(n == 3 * KT - 1))
                            n += 1
                last.then_inc(logits_done, 1)

            def turn_comb(g):
                pe.wait_ge(route_step, (g + 1) * STEPS)
                for t in range(T4):
                    last = pe.transpose(ps_misc16[0:2 * E, t * P:(t + 1) * P],
                                        comb[:, t, :, :].rearrange("p a e -> p (a e)"), ident16[:, :])
                last.then_inc(comb_turned, 1)

            def up(g, e, par, b):
                n = g * E1 + e
                if not isinstance(n, int) or n >= 2:
                    pe.wait_ge(gu_done, n - 1)
                if e == 0:
                    pe.wait_ge(x2_low, g * 2 + 2)
                for ps, w in ((ps_g[b], wg16), (ps_u[b], wu16)):
                    m = 0
                    for k in range(KT):
                        for pw, px in ((0, 0), (0, 1), (1, 0)):
                            last = pe.matmul(ps[:, :], w[:, pw, e, k, :], x2T[:, par, px, k, :],
                                             start=(m == 0), stop=(m == 3 * KT - 1))
                            m += 1
                last.then_inc(up_done, 1)

            def spread_comb(g, e):
                if e == 1:
                    pe.wait_ge(combT_ready, g + 1)
                if e > 1 or not isinstance(g, int) or g:
                    pe.wait_ge(h_done, g * E + (e - 1))
                pe.matmul(ps_comb[:, :], pick[:, e - 1, :], combT[:, :], start=True, stop=True).then_inc(cb_done, 1)

            def down(g, e):
                pe.wait_ge(h_low, g * E1 + (e + 1))
                if e == 0 and (not isinstance(g, int) or g):
                    pe.wait_ge(z2_done, 2 * g)
                for t in range(T4):
                    for m, (ph, pw) in enumerate(((0, 0), (0, 1), (1, 0))):
                        last = pe.matmul(ps_y[t // 2][:, (t % 2) * DM:(t % 2 + 1) * DM],
                                         h16[:, e % 3, ph, t * P:(t + 1) * P], wd16[:, pw, e, :],
                                         start=(e == 0 and t % 2 == 0 and m == 0),
                                         stop=(e == E1 - 1 and m == 2), skip_group_check=True)
                last.then_inc(down_done, 1)

            def group(g, par, first=False, final=False):
                for e in range(E1):
                    b = (par + e) % 2
                    if e:
                        spread_comb(g, e)
                    if e < E1 - 1:
                        up(g, e + 1, par, 1 - b)
                    elif not final:
                        up(g + 1, 0, 1 - par, 1 - b)
                    if e == 0:
                        turn_comb(g)
                        if not first:
                            down(g - 1, E1 - 1)
                    else:
                        down(g, e - 1)
                    if not final:
                        piece(e, g + 1, 1 - par)
                        if e == 7:
                            logits(g + 1, 1 - par)

            pe.sem_inc(runs_done, 1)
            pe.wait_ge(weights_ready, 1)
            for e in range(E1):
                piece(e, 0, 0)
            logits(0, 0)
            up(0, 0, 0, 0)
            group(0, 0, first=True)
            group(1, 1)
            with pe.Fori(1, G // 2 - 1) as two:
                group(two * 2, 0)
                group(two * 2 + 1, 1)
            group(G - 2, 0)
            group(G - 1, 1, final=True)
            down(G - 1, E1 - 1)

        @block.scalar
        def _(act):
            s = 0
            for tile in range(L - WARM, L):
                act.wait_ge(scan_mm, s + 1)
                if tile < L - 1:
                    nc.scalar.activation(run_state[:, s % 2, :], ps_scan[s % 2][:, 0:P], ACT.Tanh).then_inc(scan_tanh, 1)
                else:
                    nc.scalar.activation(seed[:, :, 1:NCH],
                                         ps_scan[s % 2][:, 0:P].rearrange("p (b c) -> p b c", b=NB)[:, :, 0:NCH - 1],
                                         ACT.Tanh).then_inc(scan_tanh, 1)
                s += 1
            for tile in range(L):
                act.wait_ge(scan_mm, s + 1)
                if tile < L - 1:
                    nc.scalar.activation(run_state[:, s % 2, :], ps_scan[s % 2][:, 0:P], ACT.Tanh).then_inc(scan_tanh, 1)
                else:
                    nc.scalar.activation(seed[:, :, 1:NCH],
                                         ps_scan[s % 2][:, 0:P].rearrange("p (b c) -> p b c", b=NB)[:, :, 0:NCH - 1],
                                         ACT.Tanh).then_inc(scan_tanh, 1)
                s += 1
            for tile in range(L):
                act.wait_ge(scan_mm, s + 1)
                nc.scalar.activation(states[:, tile, :], ps_scan[s % 2][:, 0:P], ACT.Tanh).then_inc(scan_tanh, 1)
                s += 1

            act.wait_ge(met_known, 1)
            runs_met = act.value_load(met[0:1, 0:1], min_val=0, max_val=1)
            with act.If(runs_met == 0):
                act.sem_inc(fb_tanh, 1)
                with act.Fori(0, NCH) as c:
                    with act.Fori(0, L // 2) as l:
                        for j in range(2):
                            act.wait_ge(fb_mm, c * L + l * 2 + (j + 1))
                            nc.scalar.activation(states[:, l * 2 + j, :].rearrange("p (b c) -> p c b", b=NB)[:, c, :],
                                                 ps_scan[j][:, 0:NB], ACT.Tanh).then_inc(fb_kept, 1)
                            nc.scalar.activation(fb_state[:, j, :], ps_scan[j][:, 0:NB], ACT.Tanh).then_inc(fb_tanh, 1)

            def piece(e, g, par):
                if e in (6, 7):
                    half = e - 6
                    act.wait_ge(x2_turned, g * 2 + half + 1)
                    nc.scalar.activation(
                        x2T[:, par, 0, :, half * 2 * P:(half + 1) * 2 * P],
                        ps_misc[:, :].rearrange("p (k t) -> p k t", k=KT), ACT.Copy, scale=XS).then_inc(x2_high, 1)
                elif e == 8:
                    act.wait_ge(logits_done, g + 1)
                    if not isinstance(g, int) or g:
                        act.wait_ge(route_step, g * STEPS)
                    nc.scalar.activation(th[:, :, :], ps_misc[:, 0:T4 * E].rearrange("p (t e) -> p t e", t=T4),
                                         ACT.Tanh, scale=l_un[:, 0:1]).then_inc(th_done, 1)

            def silu(g, e, b):
                n = g * E1 + e
                act.wait_ge(up_done, n + 1)
                if not isinstance(n, int) or n >= 2:
                    act.wait_ge(gu_done, n - 1)
                nc.scalar.activation(sg[:, b, :], ps_g[b][:, :], ACT.Silu, scale=g_un[:, 0:1]).then_inc(silu_done, 1)

            def high(g, e, b):
                n = g * E1 + e
                if e:
                    act.wait_ge(h_done, g * E + e)
                else:
                    act.wait_ge(gu_done, n + 1)
                if not isinstance(n, int) or n >= 3:
                    act.wait_ge(down_done, n - 2)
                nc.scalar.activation(h16[:, e % 3, 0, :], h[:, b, :], ACT.Copy).then_inc(h_high, 1)

            def group(g, par, final=False):
                for e in range(E1):
                    silu(g, e, (par + e) % 2)
                    high(g, e, (par + e) % 2)
                    if e == 0:
                        act.wait_ge(comb_turned, g + 1)
                        if not isinstance(g, int) or g:
                            act.wait_ge(cb_done, g * E)
                        nc.scalar.activation(combT[:, :], ps_misc16[0:2 * E, 0:GT], ACT.Copy).then_inc(combT_ready, 1)
                    if not final:
                        piece(e, g + 1, 1 - par)

            act.wait_ge(weights_ready, 1)
            for e in range(E1):
                piece(e, 0, 0)
            group(0, 0)
            group(1, 1)
            with act.Fori(1, G // 2 - 1) as two:
                group(two * 2, 0)
                group(two * 2 + 1, 1)
            group(G - 2, 0)
            group(G - 1, 1, final=True)

        @block.vector
        def _(dve):
            nc.vector.memset(seed[:, :, :], 0.0).then_inc(seed_clear, 1)
            nc.vector.memset(fb_state[:, :, :], 0.0).then_inc(seed_clear, 1)
            dve.wait_ge(mats_turned, 1)
            nc.vector.tensor_copy(AT[:, :], ps_xT[2][:, 0:P])
            nc.vector.tensor_copy(BT[:, :, :].rearrange("p k n -> p (k n)"), ps_xT[2][:, P:(KT + 1) * P]).then_inc(mats_done, 1)
            nc.vector.tensor_copy(CT[:, :, :].rearrange("p k n -> p (k n)"), ps_xT[3][:, 0:KT * P]).then_inc(mats_done, 1)
            nc.vector.tensor_copy(rwT[:, :, :].rearrange("p k n -> p (k n)"),
                                  ps_xT[3][:, KT * P:KT * P + KT * E]).then_inc(rwT_ready, 1)
            for n, pair in enumerate(pairs):
                dve.wait_ge(xT_turned, n + 1)
                nc.vector.tensor_copy(xT[:, :, pair * 2:pair * 2 + 2, :].rearrange("p k j c -> p k (j c)"),
                                      ps_xT[n % 2][:, :].rearrange("p (k j) -> p k j", k=KT)).then_inc(xT_done, 1)

            dve.wait_ge(vecs_in, 16 * NVEC)
            nc.vector.tensor_scalar(D_bc[:, :], D_bc[:, :], 1.0, None, ALU.add).then_inc(wstep, 1)
            dve.wait_ge(wstep, 1)
            for c in range(L // T4):
                dve.wait_ge(x_in[c], 16)
                nc.vector.tensor_tensor(xskip[:, c * T4:(c + 1) * T4, :], xres[:, c * T4:(c + 1) * T4, :],
                                        D_bc[:, :].unsqueeze(1).to_broadcast([P, T4, DM]), ALU.mult).then_inc(skip_done, 1)
            dve.wait_ge(w_in, 16 * NW)
            nc.vector.memset(wmax[:, :], 0.0).then_inc(wstep, 1)
            dve.wait_ge(wstep, 2)
            for i, w in enumerate((wg, wu)):
                nc.vector.tensor_reduce(wmax[:, i:i + 1], w[:, :, :, :].rearrange("p e k i -> p (e k i)"), AX_X, ALU.max,
                                        apply_absolute_value=True).then_inc(wmax_part, 1)
            nc.vector.tensor_reduce(wmax[:, 3:4], wd[:, :, :].rearrange("p e d -> p (e d)"), AX_X, ALU.max,
                                    apply_absolute_value=True).then_inc(wmax_part, 1)
            dve.wait_ge(rwT_ready, 1)
            nc.vector.tensor_reduce(wmax[:, 2:3], rwT[:, :, :].rearrange("p k e -> p (k e)"), AX_X, ALU.max,
                                    apply_absolute_value=True).then_inc(wmax_part, 1)
            dve.wait_ge(wmax_known, 1)
            nc.vector.tensor_scalar(wpow[:, :], wmax_all[:, :], 2.0 ** -60, None, ALU.max).then_inc(wstep, 1)
            dve.wait_ge(wstep, 3)
            nc.vector.tensor_scalar(wpow[:, :].bitcast(I32), wpow[:, :].bitcast(I32), 0x7F800000, None,
                                    ALU.bitwise_and).then_inc(wstep, 1)
            dve.wait_ge(wstep, 4)
            nc.vector.tensor_scalar(wscale[:, :].bitcast(I32), wpow[:, :].bitcast(I32), -1.0,
                                    float((2 * 127 + WTOP) << 23), ALU.mult, ALU.add).then_inc(wstep, 1)
            UN = 2.0 ** -WTOP / XS
            HS = 2.0 ** 15 / (DM * DM * 4)
            nc.vector.tensor_scalar(g_un[:, :], wpow[:, 0:1], UN, None, ALU.mult).then_inc(wstep, 1)
            nc.vector.tensor_scalar(l_un[:, :], wpow[:, 2:3], 0.5 * UN, None, ALU.mult).then_inc(wstep, 1)
            nc.vector.tensor_scalar(y_un[:, 1:2], wpow[:, 3:4], wpow[:, 0:1], 2.0 ** -WTOP / HS, ALU.mult, ALU.mult).then_inc(wstep, 1)
            dve.wait_ge(wstep, 8)
            nc.vector.tensor_scalar(u_un[:, 0:1], wscale[:, 0:1], 2.0 ** -WTOP * UN * HS, None, ALU.mult).then_inc(wstep, 1)
            nc.vector.tensor_scalar(u_un[:, 1:2], wscale[:, 0:1], 2.0 ** -WTOP * UN * HS / CS, None, ALU.mult).then_inc(wstep, 1)
            nc.vector.tensor_scalar(y_un[:, 0:1], y_un[:, 1:2], wpow[:, 1:2], None, ALU.mult).then_inc(wstep, 1)
            step = 11
            for i, flat, parts in (
                    (0, wg[:, :, :, :].rearrange("p e k i -> p (e k i)"), wg16[:, :, :, :, :].rearrange("p a e k i -> p a (e k i)")),
                    (1, wu[:, :, :, :].rearrange("p e k i -> p (e k i)"), wu16[:, :, :, :, :].rearrange("p a e k i -> p a (e k i)")),
                    (3, wd[:, :, :].rearrange("p e d -> p (e d)"), wd16[:, :, :, :].rearrange("p a e d -> p a (e d)"))):
                nc.vector.tensor_scalar(parts[:, 0, :], flat, wscale[:, i:i + 1], None, ALU.mult).then_inc(wstep, 1)
                step += 1
                dve.wait_ge(wstep, step)
                nc.vector.scalar_tensor_tensor(parts[:, 1, :], flat, wscale[:, i:i + 1], parts[:, 0, :],
                                               ALU.mult, ALU.subtract).then_inc(wstep, 1)
                step += 1
            flat = rwT[:, :, :].rearrange("p k e -> p (k e)")
            high, low = (rw16[:, a, :, :].rearrange("p k e -> p (k e)") for a in range(2))
            nc.vector.tensor_scalar(high, flat, wscale[:, 2:3], None, ALU.mult).then_inc(wstep, 1)
            step += 1
            dve.wait_ge(wstep, step)
            nc.vector.scalar_tensor_tensor(low, flat, wscale[:, 2:3], high, ALU.mult, ALU.subtract).then_inc(weights_ready, 1)

            dve.wait_ge(scan_tanh, WARM + 2 * L)
            nc.vector.tensor_tensor(met_diff[:, :, :],
                                    states[:, L - 1, :].rearrange("p (b c) -> p b c", b=NB)[:, :, 0:NCH - 1],
                                    seed[:, :, 1:NCH], ALU.subtract).then_inc(met_step, 1)
            dve.wait_ge(met_step, 1)
            nc.vector.tensor_reduce(met_row[:, 0:1], met_diff[:, :, :].rearrange("p b c -> p (b c)"), AX_X, ALU.max,
                                    apply_absolute_value=True).then_inc(met_part, 1)
            dve.wait_ge(met_all, 1)
            nc.vector.tensor_scalar(met[:, :], met_row[:, 1:2], MET, None, ALU.is_le).then_inc(met_known, 1)

            def stats(k, g, src, st_sem, mv_sem, t0, t1):
                for t in range(t0, t1):
                    nc.vector.bn_stats(st[:, k, t, :], src(t)).then_inc(st_sem, 1)
                dve.wait_ge(st_sem, g * T4 + t1)
                nc.vector.memset(carrier[:, :], 0.0)
                for t in range(t0, t1):
                    nc.vector.bn_aggr(mv[:, k, t, :], st[:, k, t, :]).then_inc(mv_sem, 1)

            def piece(e, g, par):
                if e in (1, 2):
                    e -= 1
                    dve.wait_ge(c_done, g * T4 + 2 * (e + 1))
                    nc.vector.tensor_tensor(y1[:, 2 * e:2 * e + 2, :], ps_misc[:, :].rearrange("p (j d) -> p j d", j=2),
                                            xskip[:, bass.ds(g * T4 + 2 * e, 2), :], ALU.add).then_inc(y1_done, 1)
                    dve.wait_ge(y1_done, g * 2 + (e + 1))
                    stats(0, g, lambda t: y1[:, t, :], st1_done, mv1_done, 2 * e, 2 * e + 2)
                elif e == 3:
                    dve.wait_ge(mv1_done, (g + 1) * T4)
                    for t in range(T4):
                        nc.vector.scalar_tensor_tensor(y1[:, t, :], y1[:, t, :], mv[:, 0, t, 0:1], gamma_bc[:, :],
                                                       ALU.subtract, ALU.mult).then_inc(scaled1, 1)
                    dve.wait_ge(rstd1_ready, g + 1)
                    for t in range(T4):
                        dve.wait_ge(scaled1, g * T4 + (t + 1))
                        nc.vector.scalar_tensor_tensor(y1[:, t, :], y1[:, t, :], rstd[:, 0, 1, t:t + 1],
                                                       xres[:, g * T4 + t, :], ALU.mult, ALU.add).then_inc(z1_done, 1)
                elif e == 4:
                    dve.wait_ge(z1_done, (g + 1) * T4)
                    stats(1, g, lambda t: y1[:, t, :], st2_done, mv2_done, 0, T4)
                elif e == 5:
                    dve.wait_ge(rstd2_ready, g + 1)
                    dve.wait_ge(mv2_done, (g + 1) * T4)
                    for t in range(T4):
                        nc.vector.tensor_scalar(x2[:, par, t, :], y1[:, t, :], mv[:, 1, t, 0:1],
                                                rstd[:, 1, 1, t:t + 1], ALU.subtract, ALU.mult).then_inc(x2_ready, 1)
                elif e in (6, 7):
                    half = e - 6
                    dve.wait_ge(x2_high, g * 2 + half + 1)
                    nc.vector.scalar_tensor_tensor(
                        x2T[:, par, 1, :, half * 2 * P:(half + 1) * 2 * P],
                        ps_misc[:, :].rearrange("p (k t) -> p k t", k=KT), XS,
                        x2T[:, par, 0, :, half * 2 * P:(half + 1) * 2 * P], ALU.mult, ALU.subtract).then_inc(x2_low, 1)

            def route(g):
                done = 0
                tt, ts = nc.vector.tensor_tensor, nc.vector.tensor_scalar

                def then(ins):
                    nonlocal done
                    done += 1
                    ins.then_inc(route_step, 1)
                    dve.wait_ge(route_step, g * STEPS + done)

                def over_experts(v):
                    return v.to_broadcast([P, T4, E])

                def first_greatest(onehot, v):
                    then(nc.vector.tensor_reduce(peak[:, :, 0], v, AX_X, ALU.max))
                    then(tt(onehot, v, over_experts(peak[:, :, 0:1]), ALU.is_equal))
                    then(tt(onehot, onehot, countdown[:, :, :], ALU.mult))
                    then(nc.vector.tensor_reduce(peak[:, :, 0], onehot, AX_X, ALU.max))
                    then(tt(onehot, onehot, over_experts(peak[:, :, 0:1]), ALU.is_equal))

                dve.wait_ge(th_done, g + 1)
                then(ts(score[:, :, :], th[:, :, :], 0.5, 0.5, ALU.mult, ALU.add))
                then(tt(choice[:, :, :], score[:, :, :], cbias_bc[:, :].unsqueeze(1).to_broadcast([P, T4, E]), ALU.add))
                by2 = choice[:, :, :].rearrange("p t (q a) -> p t q a", a=2)
                tt(more[:, :, :], by2[:, :, :, 0], by2[:, :, :, 1], ALU.max)
                then(tt(less[:, :, :], by2[:, :, :, 0], by2[:, :, :, 1], ALU.min))
                more2 = more[:, :, :].rearrange("p t (q a) -> p t q a", a=2)
                less2 = less[:, :, :].rearrange("p t (q a) -> p t q a", a=2)
                tt(top[:, :, :], more2[:, :, :, 0], more2[:, :, :, 1], ALU.max)
                tt(second[:, :, :], more2[:, :, :, 0], more2[:, :, :, 1], ALU.min)
                then(tt(other[:, :, :], less2[:, :, :, 0], less2[:, :, :, 1], ALU.max))
                then(tt(second[:, :, :], second[:, :, :], other[:, :, :], ALU.max))
                then(tt(top[:, :, :], top[:, :, :], second[:, :, :], ALU.add))
                tt(mask[:, :, 0:1], top[:, :, 0:1], top[:, :, 1:2], ALU.is_ge)
                then(tt(mask[:, :, 1:2], top[:, :, 0:1], top[:, :, 1:2], ALU.is_lt))
                by_group = choice[:, :, :].rearrange("p t (q a) -> p t q a", q=2)
                then(tt(by_group, by_group, mask[:, :, :].unsqueeze(3).to_broadcast([P, T4, 2, EPG]), ALU.mult))
                first_greatest(pick1[:, :, :], choice[:, :, :])
                then(nc.vector.scalar_tensor_tensor(choice[:, :, :], pick1[:, :, :], -1e30, choice[:, :, :], ALU.mult, ALU.add))
                first_greatest(pick2[:, :, :], choice[:, :, :])
                then(tt(pick1[:, :, :], pick1[:, :, :], pick2[:, :, :], ALU.add))
                then(tt(pick1[:, :, :], pick1[:, :, :], score[:, :, :], ALU.mult))
                then(nc.vector.tensor_reduce(peak[:, :, 0], pick1[:, :, :], AX_X, ALU.add))
                then(ts(peak[:, :, 1], peak[:, :, 0], 1e-20, 1.0 / CS, ALU.add, ALU.mult))
                then(nc.vector.reciprocal(peak[:, :, 0], peak[:, :, 1]))
                then(tt(pick1[:, :, :], pick1[:, :, :], over_experts(peak[:, :, 0:1]), ALU.mult))
                if not isinstance(g, int) or g:
                    dve.wait_ge(comb_turned, g)
                then(nc.vector.tensor_copy(comb[:, :, 0, :], pick1[:, :, :]))
                then(tt(comb[:, :, 1, :], pick1[:, :, :], comb[:, :, 0, :], ALU.subtract))
                assert done == STEPS, done

            def inner(g, e, b):
                n = g * E1 + e
                dve.wait_ge(silu_done, n + 1)
                if not isinstance(n, int) or n >= 2:
                    dve.wait_ge(h_low, n - 1)
                if e == 0:
                    nc.vector.scalar_tensor_tensor(h[:, b, :], ps_u[b][:, :], u_un[:, 0:1], sg[:, b, :],
                                                   ALU.mult, ALU.mult).then_inc(gu_done, 1)
                else:
                    nc.vector.scalar_tensor_tensor(gu[:, b, :], ps_u[b][:, :], u_un[:, 1:2], sg[:, b, :],
                                                   ALU.mult, ALU.mult).then_inc(gu_done, 1)
                    dve.wait_ge(gu_done, n + 1)
                    dve.wait_ge(cb_done, g * E + e)
                    nc.vector.tensor_tensor(h[:, b, :], ps_comb[:, :], gu[:, b, :], ALU.mult).then_inc(h_done, 1)

            def close(step, g, par):
                if step == 0:
                    dve.wait_ge(down_done, (g + 1) * E1)
                    for j in range(2):
                        part = x2[:, par, 2 * j:2 * j + 2, :]
                        nc.vector.scalar_tensor_tensor(part, ps_y[j][:, :].rearrange("p (j d) -> p j d", j=2), y_un[:, 0:1],
                                                       part, ALU.mult, ALU.add).then_inc(z2_done, 1)
                elif step == 1:
                    dve.wait_ge(z2_done, (g + 1) * 2)
                    stats(2, g, lambda t: x2[:, par, t, :], st3_done, mv3_done, 0, T4)
                else:
                    dve.wait_ge(rstd3_ready, g + 1)
                    dve.wait_ge(mv3_done, (g + 1) * T4)
                    for t in range(T4):
                        nc.vector.tensor_scalar(xskip[:, g * T4 + t, :], x2[:, par, t, :], mv[:, 2, t, 0:1],
                                                rstd[:, 2, 1, t:t + 1], ALU.subtract, ALU.mult).then_inc(out_ready, 1)

            def group(g, par, first=False, final=False):
                for e in range(E1):
                    inner(g, e, (par + e) % 2)
                    if not final:
                        piece(e, g + 1, 1 - par)
                        if e == E1 - 1:
                            route(g + 1)
                    if e in (0, 1, 2) and not first:
                        close(e, g - 1, 1 - par)

            dve.wait_ge(res_done, L // T4)
            dve.wait_ge(skip_done, L // T4)
            for e in range(E1):
                piece(e, 0, 0)
            route(0)
            group(0, 0, first=True)
            group(1, 1)
            with dve.Fori(1, G // 2 - 1) as two:
                group(two * 2, 0)
                group(two * 2 + 1, 1)
            group(G - 2, 0)
            group(G - 1, 1, final=True)
            close(0, G - 1, 1)
            close(1, G - 1, 1)
            close(2, G - 1, 1)

        @block.gpsimd
        def _(pool):
            nc.gpsimd.memset(ident[:, :], 0.0).then_inc(const_step, 1)
            pool.wait_ge(const_step, 1)
            nc.gpsimd.affine_select(out=ident[:, :], in_=ident[:, :], compare_op=ALU.not_equal, fill=1.0, base=0,
                                    pattern=[[-1, P]], channel_multiplier=1).then_inc(consts, 1)
            pool.wait_ge(consts, 1)
            nc.gpsimd.tensor_copy(ident16[:, :], ident[:, :]).then_inc(consts, 1)
            nc.gpsimd.memset(pick[:, :, :], 0.0).then_inc(const_step, 1)
            pool.wait_ge(const_step, 2)
            for a in range(2):
                nc.gpsimd.affine_select(out=pick[:, :, :], in_=pick[:, :, :], compare_op=ALU.not_equal, fill=1.0,
                                        base=-a * E, pattern=[[-1, E], [0, P]], channel_multiplier=1).then_inc(const_step, 1)
                pool.wait_ge(const_step, 3 + a)
            for e in range(E):
                nc.gpsimd.memset(countdown[:, :, e:e + 1], float(E - e))
            nc.gpsimd.memset(eps[:, :], LN_EPS)
            nc.gpsimd.memset(neghalf[:, :], -0.5).then_inc(const_step, 1)
            pool.wait_ge(const_step, 5)
            pool.wait_ge(vecs_in, 16 * NVEC)
            pool.wait_ge(wmax_part, 4)
            nc.gpsimd.partition_all_reduce(wmax_all[:, :], wmax[:, :], P, RMAX).then_inc(wmax_known, 1)
            pool.wait_ge(xT_turned, len(pairs))
            for c in range(L // T4):
                pool.wait_ge(skip_done, c + 1)
                nc.gpsimd.tensor_tensor(xres[:, c * T4:(c + 1) * T4, :], xres[:, c * T4:(c + 1) * T4, :],
                                        beta_bc[:, :].unsqueeze(1).to_broadcast([P, T4, DM]), ALU.add).then_inc(res_done, 1)
            pool.wait_ge(met_part, 1)
            nc.gpsimd.partition_all_reduce(met_row[:, 1:2], met_row[:, 0:1], P, RMAX).then_inc(met_all, 1)

            def copy_states(g):
                if not isinstance(g, int) or g:
                    pool.wait_ge(c_done, g * T4)
                nc.gpsimd.tensor_copy(gstates[:, :, :], states[:, bass.ds(g * T4, T4), :]).then_inc(gstates_ready, 1)

            def rsqrt(k, g, mv_sem, ready, count):
                pool.wait_ge(mv_sem, (g + 1) * T4)
                nc.gpsimd.tensor_tensor(rstd[:, k, 0, :], mv[:, k, :, 1], eps[:, :], ALU.add).then_inc(rstd_step, 1)
                pool.wait_ge(rstd_step, count + 1)
                nc.gpsimd.tensor_tensor(rstd[:, k, 1, :], rstd[:, k, 0, :], neghalf[:, :], ALU.pow).then_inc(ready, 1)

            def low(g, e, b):
                pool.wait_ge(h_high, g * E1 + (e + 1))
                nc.gpsimd.tensor_tensor(h16[:, e % 3, 1, :], h[:, b, :], h16[:, e % 3, 0, :], ALU.subtract).then_inc(h_low, 1)

            pool.wait_ge(runs_done, 1)
            copy_states(0)
            rsqrt(0, 0, mv1_done, rstd1_ready, 0)
            rsqrt(1, 0, mv2_done, rstd2_ready, 1)

            def group(g, par, first=False, final=False):
                count = g * 3 + (2 if first else 1)
                if not final:
                    copy_states(g + 1)
                for e in range(E1):
                    low(g, e, (par + e) % 2)
                    if e == 1 and not first:
                        rsqrt(2, g - 1, mv3_done, rstd3_ready, count)
                    elif e == 2 and not final:
                        rsqrt(0, g + 1, mv1_done, rstd1_ready, count + (0 if first else 1))
                    elif e == 4 and not final:
                        rsqrt(1, g + 1, mv2_done, rstd2_ready, count + (1 if first else 2))

            group(0, 0, first=True)
            group(1, 1)
            with pool.Fori(1, G // 2 - 1) as two:
                group(two * 2, 0)
                group(two * 2 + 1, 1)
            group(G - 2, 0)
            group(G - 1, 1, final=True)
            rsqrt(2, G - 1, mv3_done, rstd3_ready, (G - 1) * 3 + 2)


_INS = ["L0_attn_x", "L0_attn_A", "L0_attn_B", "L0_attn_C", "L0_attn_D", "L0_attn_gamma", "L0_attn_beta",
        "L0_ffn_router_weight", "L0_ffn_correction_bias", "L0_ffn_w_gate", "L0_ffn_w_up", "L0_ffn_w_down",
        "L0_ffn_sw_gate", "L0_ffn_sw_up", "L0_ffn_sw_down"]


def kernel(**inputs):
    import numpy as np
    import concourse.bacc as bacc
    from concourse.bass_utils import run_bass_kernel_spmd

    nc = bacc.Bacc("TRN2", target_bir_lowering=False, num_devices=1)
    arrays, args = {}, []
    for name in _INS:
        a = np.ascontiguousarray(inputs[name])
        arrays[f"in_{name}_dram"] = a
        args.append(nc.dram_tensor(f"in_{name}_dram", a.shape, mybir.dt.from_np(a.dtype), kind="ExternalInput").ap())
    shape = inputs["L0_attn_x"].shape
    args.append(nc.dram_tensor("out_0_dram", shape, F32, kind="ExternalOutput").ap())
    ssm_moe_kernel(nc, *args)
    r = run_bass_kernel_spmd(nc, [arrays], core_ids=[0])
    return r.results[0]["out_0_dram"]
```

```python
from contextlib import ExitStack

import concourse.bass as bass
from concourse import mybir

ALU = mybir.AluOpType
ACT = mybir.ActivationFunctionType
F32 = mybir.dt.float32
F16 = mybir.dt.float16
I32 = mybir.dt.int32
AX_X = mybir.AxisListType.X
RMAX = bass.bass_isa.ReduceOp.max
P = 128

LN_EPS = 1e-5
MET = 2.0 ** -20


def ssm_moe_kernel(nc, x, A, B, C, D, gamma, beta, router_weight, correction_bias,
                   w_gate, w_up, w_down, sw_gate, sw_up, sw_down, out):
    NB, S, DM = x.shape
    NS = A.shape[0]
    E, _, I = w_gate.shape
    KT = DM // P
    L = NB * S // P
    NCH = P // NB
    WARM = 4
    T4 = 4
    G = L // T4
    GT = T4 * P
    E1 = E + 1
    EPG = E // 2
    assert NS == P and I == P and DM == 2 * P and L % (2 * T4) == 0

    XS = 2.0 ** 11
    WTOP = 14
    CS = 2.0 ** 14

    with ExitStack() as ctx:
        def sb(name, shape, dt=F32):
            return ctx.enter_context(nc.sbuf_tensor(name, shape, dt))

        def sem(name):
            return ctx.enter_context(nc.semaphore(name))

        xres = sb("xres", [P, L, DM])
        xskip = sb("xskip", [P, L, DM])
        xT = sb("xT", [P, KT, L, P])
        states = sb("states", [P, L, P])
        run_state = sb("run_state", [P, 2, P])
        seed = sb("seed", [P, NB, NCH])
        fb_state = sb("fb_state", [P, 2, NB])
        met_diff = sb("met_diff", [P, NB, NCH - 1])
        met_row = sb("met_row", [P, 2])
        met = sb("met", [P, 1], I32)
        act_warm = sb("act_warm", [P, 1])

        ident = sb("ident", [P, P])
        ident16 = sb("ident16", [P, P], F16)
        A_sb = sb("A_sb", [P, NS])
        B_sb = sb("B_sb", [P, DM])
        C_sb = sb("C_sb", [P, KT, NS])
        rw_sb = sb("rw_sb", [E, DM])
        AT = sb("AT", [P, NS])
        BT = sb("BT", [P, KT, NS])
        CT = sb("CT", [P, KT, P])
        rwT = sb("rwT", [P, KT, E])
        rw16 = sb("rw16", [P, 2, KT, E], F16)
        D_bc = sb("D_bc", [P, DM])
        gamma_bc = sb("gamma_bc", [P, DM])
        beta_bc = sb("beta_bc", [P, DM])
        cbias_bc = sb("cbias_bc", [P, E])

        wg = sb("wg", [P, E1, KT, I])
        wu = sb("wu", [P, E1, KT, I])
        wd = sb("wd", [P, E1, DM])
        wg16 = sb("wg16", [P, 2, E1, KT, I], F16)
        wu16 = sb("wu16", [P, 2, E1, KT, I], F16)
        wd16 = sb("wd16", [P, 2, E1, DM], F16)
        wmax = sb("wmax", [P, 4])
        wmax_all = sb("wmax_all", [P, 4])
        wpow = sb("wpow", [P, 4])
        wscale = sb("wscale", [P, 4])
        g_un = sb("g_un", [P, 1])
        u_un = sb("u_un", [P, 2])
        l_un = sb("l_un", [P, 1])
        y_un = sb("y_un", [P, 2])

        late = xT[:, :, :, :].rearrange("p k l c -> p (k l c)")
        sg, gu, h = (late[:, i * 2 * GT:(i + 1) * 2 * GT].rearrange("p (b t) -> p b t", b=2) for i in range(3))
        gstates = late[:, 6 * GT:7 * GT].rearrange("p (t c) -> p t c", t=T4)
        x2 = wg[:, :, :, :].rearrange("p e k i -> p (e k i)")[:, 0:2 * T4 * DM].rearrange("p (a t d) -> p a t d", a=2, t=T4)
        y1 = wu[:, :, :, :].rearrange("p e k i -> p (e k i)")[:, 0:T4 * DM].rearrange("p (t d) -> p t d", t=T4)
        st = sb("st", [P, 3, T4, 6])
        mv = sb("mv", [P, 3, T4, 2])
        rstd = sb("rstd", [P, 3, 2, T4])
        neghalf = sb("neghalf", [P, T4])
        carrier = sb("carrier", [P, 1])
        eps = sb("eps", [P, T4])
        x2T = sb("x2T", [P, 2, 2, KT, GT], F16)
        th = sb("th", [P, T4, E])
        score = sb("score", [P, T4, E])
        choice = sb("choice", [P, T4, E])
        more, both = sb("more", [P, T4, E // 2]), sb("both", [P, T4, E // 2])
        top, across, mask, total = (sb(n, [P, T4, 2]) for n in ("top", "across", "mask", "total"))
        ahead, level = sb("ahead", [P, T4, E, E]), sb("level", [P, T4, E, E])
        lower = sb("lower", [P, E, E])
        rank, kept = sb("rank", [P, T4, E]), sb("kept", [P, T4, E])
        h16 = sb("h16", [P, 3, 2, GT], F16)
        comb = sb("comb", [P, T4, 2, E], F16)
        combT = sb("combT", [2 * E, GT], F16)
        pick = sb("pick", [2 * E, E, P], F16)

        bank = [ctx.enter_context(nc.psum_tensor(f"bank{i}", [P, 512], F32)) for i in range(8)]
        ps_scan = bank[4:6]
        ps_xT, ps_mats = bank[0:4], bank[6:8]
        ps_g, ps_u, ps_y = bank[0:2], bank[2:4], bank[4:6]
        ps_comb, ps_misc = bank[6], bank[7]
        ps_misc16 = ps_misc[:, :].bitcast(F16)

        x_in = [sem(f"x_in{i}") for i in range(L // T4)]
        AB_in, Cr_in, vecs_in = sem("AB_in"), sem("Cr_in"), sem("vecs_in")
        w_in = [sem(f"w_in{i}") for i in range(3)]
        const_step, consts = sem("const_step"), sem("consts")
        AB_turned, AB_done, Cr_turned, Cr_done = sem("AB_turned"), sem("AB_done"), sem("Cr_turned"), sem("Cr_done")
        xT_turned, xT_first, xT_done = sem("xT_turned"), sem("xT_first"), sem("xT_done")
        seed_clear, scan_mm, scan_tanh = sem("seed_clear"), sem("scan_mm"), sem("scan_tanh")
        met_step, met_part, met_all, met_known = sem("met_step"), sem("met_part"), sem("met_all"), sem("met_known")
        fb_mm, fb_tanh, fb_kept = sem("fb_mm"), sem("fb_tanh"), sem("fb_kept")
        runs_done = sem("runs_done")
        skip_done, res_done = sem("skip_done"), sem("res_done")
        wmax_part, wmax_known, wstep, weights_ready = sem("wmax_part"), sem("wmax_known"), sem("wstep"), sem("weights_ready")
        w_high = [sem(f"w_high{i}") for i in range(4)]

        def ahead_sems(prefix):
            names = ("c_done y1_done st1_done mv1_done scaled1 z1_done st2_done mv2_done x2_ready "
                     "rstd1_ready rstd2_ready x2_turned x2_high x2_low logits_done th_done choice_step").split()
            return {name: sem(prefix + name) for name in names}

        main, again = ahead_sems(""), ahead_sems("again_")
        again_up, again_rstd_step = sem("again_up"), sem("again_rstd_step")
        gstates_ready, rstd_step, rstd3_ready = sem("gstates_ready"), sem("rstd_step"), sem("rstd3_ready")
        route_step, comb_turned, combT_ready = sem("route_step"), sem("comb_turned"), sem("combT_ready")
        up_done, silu_done, gu_done, cb_done, h_done, h_high, h_low, down_done = (
            sem("up_done"), sem("silu_done"), sem("gu_done"), sem("cb_done"), sem("h_done"),
            sem("h_high"), sem("h_low"), sem("down_done"))
        z2_done, st3_done, mv3_done, out_ready, out_sent = (
            sem("z2_done"), sem("st3_done"), sem("mv3_done"), sem("out_ready"), sem("out_sent"))

        x_dram = x.rearrange("b s d -> (b s) d").rearrange("(p l) d -> p l d", l=L)
        out_dram = out.rearrange("b s d -> (b s) d").rearrange("(p l) d -> p l d", l=L)

        chunks = [L // T4 - 1] + list(range(L // T4 - 1))
        pairs = [c * T4 // 2 + j for c in chunks for j in range(T4 // 2)]
        WEIGHT_LOADS = [
            (w_gate.rearrange("e (k p) i -> p (e k) i", p=P), wg[:, 1:E1, :, :].rearrange("p e k i -> p (e k) i"),
             sw_gate.rearrange("(k p) i -> p k i", p=P), wg[:, 0, :, :]),
            (w_up.rearrange("e (k p) i -> p (e k) i", p=P), wu[:, 1:E1, :, :].rearrange("p e k i -> p (e k) i"),
             sw_up.rearrange("(k p) i -> p k i", p=P), wu[:, 0, :, :]),
            (w_down.rearrange("e i d -> i e d"), wd[:, 1:E1, :], sw_down, wd[:, 0, :])]
        NVEC = 4
        FIRST = 2
        HALVES = 2 * (len(pairs) - FIRST)
        PE_AT = {1: (0, 0), 2: (0, 1), 5: (1, 0), 6: (1, 1), 18: (5, 0), 19: (5, 1), 22: (6, 0), 23: (6, 1),
                 26: (7, 0), 27: (7, 1)}
        ACT_AT = {20: 6, 24: 7, 28: 8}
        UP_FROM = 28
        NUP = 2 * 3 * KT
        CHOICE_STEPS, STEPS = 10, 8

        block = ctx.enter_context(nc.Block())

        @block.sync
        def _(sp):
            def load_x(n):
                c = chunks[n]
                sp.dma_start(xres[:, c * T4:(c + 1) * T4, :], x_dram[:, c * T4:(c + 1) * T4, :]).then_inc(x_in[c], 16)

            def load_weights(i):
                routed, to_routed, shared, to_shared = WEIGHT_LOADS[i]
                sp.dma_start(to_routed, routed).then_inc(w_in[i], 16)
                sp.dma_start(to_shared, shared).then_inc(w_in[i], 16)

            sp.dma_start(A_sb[:, :], A).then_inc(AB_in, 16)
            sp.dma_start(B_sb[:, :], B).then_inc(AB_in, 16)
            load_x(0)
            load_x(1)
            sp.dma_start(C_sb[:, :, :], C.rearrange("(k p) n -> p k n", p=P)).then_inc(Cr_in, 16)
            sp.dma_start(rw_sb[:, :], router_weight).then_inc(Cr_in, 16)
            load_x(2)
            sp.dma_start(D_bc[:, :], D.partition_broadcast(P)).then_inc(vecs_in, 16)
            sp.dma_start(gamma_bc[:, :], gamma.partition_broadcast(P)).then_inc(vecs_in, 16)
            sp.dma_start(beta_bc[:, :], beta.partition_broadcast(P)).then_inc(vecs_in, 16)
            sp.dma_start(cbias_bc[:, :], correction_bias.partition_broadcast(P)).then_inc(vecs_in, 16)
            load_x(3)
            for i in range(3):
                load_weights(i)
                load_x(4 + i)
            load_x(7)

            def send(g):
                sp.wait_ge(out_ready, (g + 1) * T4)
                sp.dma_start(out_dram[:, bass.ds(g * T4, T4), :], xskip[:, bass.ds(g * T4, T4), :]).then_inc(out_sent, 16)

            with sp.Fori(0, G) as g:
                send(g)
            sp.wait_ge(out_sent, 16 * G)

        @block.tensor
        def _(pe):
            pe.wait_ge(consts, 2)
            pe.wait_ge(AB_in, 16 * 2)
            pe.transpose(ps_mats[0][:, 0:P], A_sb[:, :], ident[:, :])
            for k in range(KT):
                last = pe.transpose(ps_mats[0][:, (k + 1) * P:(k + 2) * P], B_sb[:, k * P:(k + 1) * P], ident[:, :])
            last.then_inc(AB_turned, 1)

            def turn_Cr():
                pe.wait_ge(Cr_in, 16 * 2)
                for k in range(KT):
                    pe.transpose(ps_mats[1][:, k * P:(k + 1) * P], C_sb[:, k, :], ident[:, :])
                for k in range(KT):
                    last = pe.transpose(ps_mats[1][:, KT * P + k * E:KT * P + (k + 1) * E], rw_sb[:, k * P:(k + 1) * P],
                                        ident[0:E, 0:E])
                last.then_inc(Cr_turned, 1)

            def turn_x(n, k):
                pair = pairs[n]
                pe.wait_ge(x_in[pair * 2 // T4], 16)
                for j in range(2):
                    last = pe.transpose(ps_xT[(2 * n + k) % 4][:, j * P:(j + 1) * P],
                                        xres[:, pair * 2 + j, k * P:(k + 1) * P], ident[:, :])
                last.then_inc(xT_turned, 1)

            def drive(s, tile):
                if s % 2 == 0 and s < 2 * FIRST:
                    pe.wait_ge(xT_first, s + 2)
                elif s % 2 == 0 and s < L:
                    pe.wait_ge(xT_done, s - 2 * FIRST + 2)
                for k in range(KT):
                    pe.matmul(ps_scan[s % 2][:, 0:P], BT[:, k, :], xT[:, k, tile, :], start=(k == 0), stop=False)

            def scan_step(s, tiles, before):
                if s:
                    pe.wait_ge(scan_tanh, s)
                pe.matmul(ps_scan[s % 2][:, 0:P], AT[:, :], before, start=False, stop=True).then_inc(scan_mm, 1)
                if s + 1 < len(tiles):
                    drive(s + 1, tiles[s + 1])

            for n in range(FIRST):
                for k in range(KT):
                    turn_x(n, k)
            pe.wait_ge(AB_done, 1)
            pe.wait_ge(seed_clear, 2)
            seeds = seed[:, :, :].rearrange("p b c -> p (b c)")
            tiles = list(range(L - WARM, L)) + 2 * list(range(L))
            drive(0, tiles[0])
            for s in range(WARM + L):
                scan_step(s, tiles, seeds if s in (0, WARM) else run_state[:, (s - 1) % 2, :])
                if s < HALVES:
                    turn_x(FIRST + s // 2, s % 2)
                if s == WARM:
                    turn_Cr()

            def piece(e, g, par, sems, halves=(0, 1)):
                for half in halves:
                    if e in (0, 1):
                        if half == 0 and e == 1:
                            pe.wait_ge(sems["y1_done"], g * 2 + 1)
                        elif half == 0 and (not isinstance(g, int) or g):
                            pe.wait_ge(combT_ready, g)
                        elif half == 0:
                            pe.wait_ge(Cr_done, 2)
                        if not isinstance(g, int) or g:
                            pe.wait_ge(gstates_ready, g)
                            src = gstates
                        else:
                            src = states
                        pe.matmul(ps_misc[:, half * DM:(half + 1) * DM], src[:, 2 * e + half, :],
                                  CT[:, :, :].rearrange("p k d -> p (k d)"), start=True, stop=True).then_inc(sems["c_done"], 1)
                    elif e in (5, 6):
                        if half == 0 and e == 5:
                            pe.wait_ge(sems["x2_ready"], g * T4 + 2)
                        elif half == 0:
                            pe.wait_ge(sems["x2_low"], g * 2 + 1)
                        for j in range(2):
                            pe.transpose(ps_misc[:, (half * 2 + j) * P:(half * 2 + j + 1) * P],
                                         x2[:, par, 2 * (e - 5) + j, half * P:(half + 1) * P],
                                         ident[:, :]).then_inc(sems["x2_turned"], 1)
                    elif e == 7:
                        if half == 0:
                            pe.wait_ge(sems["x2_low"], g * 2 + 2)
                        for t in (2 * half, 2 * half + 1):
                            n = 0
                            for px, pw in ((0, 0), (0, 1), (1, 0)):
                                for k in range(KT):
                                    last = pe.matmul(ps_misc[:, t * E:(t + 1) * E], x2T[:, par, px, k, t * P:(t + 1) * P],
                                                     rw16[:, pw, k, :], start=(n == 0), stop=(n == 3 * KT - 1))
                                    n += 1
                            last.then_inc(sems["logits_done"], 1)

            def up_products(e, par, b, of=range(NUP)):
                for n in of:
                    ps, w = ((ps_g[b], wg16), (ps_u[b], wu16))[n // (NUP // 2)]
                    m = n % (NUP // 2)
                    pw, px = ((0, 0), (0, 1), (1, 0))[m % 3]
                    last = pe.matmul(ps[:, :], w[:, pw, e, m // 3, :], x2T[:, par, px, m // 3, :],
                                     start=(m == 0), stop=(m == NUP // 2 - 1))
                return last

            def up(g, e, par, b):
                n = g * E1 + e
                if not isinstance(n, int) or n >= 2:
                    pe.wait_ge(gu_done, n - 1)
                if e == 0:
                    pe.wait_ge(main["x2_low"], g * 2 + 2)
                up_products(e, par, b).then_inc(up_done, 1)

            n_up = 0
            for i in range(L):
                s = WARM + L + i
                scan_step(s, tiles, seeds if i == 0 else states[:, i - 1, :])
                if i in PE_AT:
                    e, half = PE_AT[i]
                    piece(e, 0, 0, main, halves=(half,))
                if i == UP_FROM:
                    pe.wait_ge(weights_ready, 4)
                if i >= UP_FROM:
                    up_products(0, 0, 0, of=(n_up, n_up + 1))
                    n_up += 2
            up_products(0, 0, 0, of=range(n_up, NUP)).then_inc(up_done, 1)
            up(0, 1, 0, 1)

            pe.wait_ge(met_known, 1)
            runs_met = pe.value_load(met[0:1, 0:1], min_val=0, max_val=1)
            with pe.If(runs_met == 0):
                with pe.Fori(0, NCH) as c:
                    with pe.Fori(0, L // 2) as l:
                        for j in range(2):
                            for k in range(KT):
                                pe.matmul(ps_scan[j][:, 0:NB], BT[:, k, :],
                                                 xT[:, k, l * 2 + j, :].rearrange("p (b c) -> p c b", b=NB)[:, c, :],
                                                 start=(k == 0), stop=False)
                            pe.wait_ge(fb_tanh, c * L + l * 2 + (j + 1))
                            pe.matmul(ps_scan[j][:, 0:NB], AT[:, :], fb_state[:, 1 - j, :],
                                      start=False, stop=True).then_inc(fb_mm, 1)
                pe.wait_ge(fb_kept, NCH * L)
                for e in range(E1):
                    piece(e, 0, 0, again)
                for e in range(2):
                    up_products(e, 0, e).then_inc(again_up, 1)
            pe.sem_inc(runs_done, 1)

            def turn_comb(g):
                pe.wait_ge(route_step, (g + 1) * STEPS)
                for t in range(T4):
                    last = pe.transpose(ps_misc16[0:2 * E, t * P:(t + 1) * P],
                                        comb[:, t, :, :].rearrange("p a e -> p (a e)"), ident16[:, :])
                last.then_inc(comb_turned, 1)

            def spread_comb(g, e):
                if e == 1:
                    pe.wait_ge(combT_ready, g + 1)
                if e > 1 or not isinstance(g, int) or g:
                    pe.wait_ge(h_done, g * E + (e - 1))
                pe.matmul(ps_comb[:, :], pick[:, e - 1, :], combT[:, :], start=True, stop=True).then_inc(cb_done, 1)

            def down(g, e):
                pe.wait_ge(h_low, g * E1 + (e + 1))
                if e == 0 and (not isinstance(g, int) or g):
                    pe.wait_ge(z2_done, 2 * g)
                for t in range(T4):
                    for m, (ph, pw) in enumerate(((0, 0), (0, 1), (1, 0))):
                        last = pe.matmul(ps_y[t // 2][:, (t % 2) * DM:(t % 2 + 1) * DM],
                                         h16[:, e % 3, ph, t * P:(t + 1) * P], wd16[:, pw, e, :],
                                         start=(e == 0 and t % 2 == 0 and m == 0),
                                         stop=(e == E1 - 1 and m == 2), skip_group_check=True)
                last.then_inc(down_done, 1)

            def group(g, par, first=False, final=False):
                for e in range(E1):
                    b = (par + e) % 2
                    if e:
                        spread_comb(g, e)
                    if e < E1 - 1:
                        if e or not first:
                            up(g, e + 1, par, 1 - b)
                    elif not final:
                        up(g + 1, 0, 1 - par, 1 - b)
                    if e:
                        down(g, e - 1)
                    else:
                        turn_comb(g)
                        if not first:
                            down(g - 1, E1 - 1)
                    if not final:
                        piece(e, g + 1, 1 - par, main)

            group(0, 0, first=True)
            group(1, 1)
            with pe.Fori(1, G // 2 - 1) as two:
                group(two * 2, 0)
                group(two * 2 + 1, 1)
            group(G - 2, 0)
            group(G - 1, 1, final=True)
            down(G - 1, E1 - 1)

        @block.scalar
        def _(act):
            def piece(e, g, par, sems):
                if e in (6, 7):
                    half = e - 6
                    act.wait_ge(sems["x2_turned"], g * 8 + 4 * (half + 1))
                    nc.scalar.activation(
                        x2T[:, par, 0, :, half * 2 * P:(half + 1) * 2 * P],
                        ps_misc[:, :].rearrange("p (k t) -> p k t", k=KT), ACT.Copy, scale=XS).then_inc(sems["x2_high"], 1)
                elif e == 8:
                    act.wait_ge(sems["logits_done"], (g + 1) * T4)
                    if not isinstance(g, int) or g:
                        act.wait_ge(sems["choice_step"], g * CHOICE_STEPS)
                    nc.scalar.activation(th[:, :, :], ps_misc[:, 0:T4 * E].rearrange("p (t e) -> p t e", t=T4),
                                         ACT.Tanh, scale=l_un[:, 0:1]).then_inc(sems["th_done"], 1)

            act.wait_ge(seed_clear, 1)
            nc.scalar.activation(act_warm[:, :], seed[:, 0, 0:1], ACT.Silu)

            def step(s, dst):
                act.wait_ge(scan_mm, s + 1)
                nc.scalar.activation(dst, ps_scan[s % 2][:, 0:P], ACT.Tanh).then_inc(scan_tanh, 1)

            for s in range(WARM + L):
                if s in (WARM - 1, WARM + L - 1):
                    act.wait_ge(scan_mm, s + 1)
                    nc.scalar.activation(seed[:, :, 1:NCH],
                                         ps_scan[s % 2][:, 0:P].rearrange("p (b c) -> p b c", b=NB)[:, :, 0:NCH - 1],
                                         ACT.Tanh).then_inc(scan_tanh, 1)
                else:
                    step(s, run_state[:, s % 2, :])
                if 1 <= s <= HALVES:
                    n, k = FIRST + (s - 1) // 2, (s - 1) % 2
                    act.wait_ge(xT_turned, 2 * FIRST + s)
                    nc.scalar.activation(xT[:, k, pairs[n] * 2:pairs[n] * 2 + 2, :].rearrange("p j c -> p (j c)"),
                                         ps_xT[(2 * n + k) % 4][:, 0:2 * P], ACT.Copy).then_inc(xT_done, 1)
            for i in range(L):
                step(WARM + L + i, states[:, i, :])
                if i in ACT_AT:
                    piece(ACT_AT[i], 0, 0, main)

            act.wait_ge(met_known, 1)
            runs_met = act.value_load(met[0:1, 0:1], min_val=0, max_val=1)
            with act.If(runs_met == 0):
                act.sem_inc(fb_tanh, 1)
                with act.Fori(0, NCH) as c:
                    with act.Fori(0, L // 2) as l:
                        for j in range(2):
                            act.wait_ge(fb_mm, c * L + l * 2 + (j + 1))
                            nc.scalar.activation(states[:, l * 2 + j, :].rearrange("p (b c) -> p c b", b=NB)[:, c, :],
                                                 ps_scan[j][:, 0:NB], ACT.Tanh).then_inc(fb_kept, 1)
                            nc.scalar.activation(fb_state[:, j, :], ps_scan[j][:, 0:NB], ACT.Tanh).then_inc(fb_tanh, 1)
                for e in range(E1):
                    piece(e, 0, 0, again)
                act.wait_ge(again_up, 2)

            def silu(g, e, b):
                n = g * E1 + e
                act.wait_ge(up_done, n + 1)
                if not isinstance(n, int) or n >= 2:
                    act.wait_ge(gu_done, n - 1)
                nc.scalar.activation(sg[:, b, :], ps_g[b][:, :], ACT.Silu, scale=g_un[:, 0:1]).then_inc(silu_done, 1)

            def high(g, e, b):
                n = g * E1 + e
                if e:
                    act.wait_ge(h_done, g * E + e)
                else:
                    act.wait_ge(gu_done, n + 1)
                if not isinstance(n, int) or n >= 3:
                    act.wait_ge(down_done, n - 2)
                nc.scalar.activation(h16[:, e % 3, 0, :], h[:, b, :], ACT.Copy).then_inc(h_high, 1)

            def group(g, par, final=False):
                for e in range(E1):
                    silu(g, e, (par + e) % 2)
                    if e == E1 - 1 and not final:
                        piece(e, g + 1, 1 - par, main)
                    if e == 0:
                        act.wait_ge(comb_turned, g + 1)
                        if not isinstance(g, int) or g:
                            act.wait_ge(cb_done, g * E)
                        nc.scalar.activation(combT[:, :], ps_misc16[0:2 * E, 0:GT], ACT.Copy).then_inc(combT_ready, 1)
                    high(g, e, (par + e) % 2)
                    if e < E1 - 1 and not final:
                        piece(e, g + 1, 1 - par, main)

            group(0, 0)
            group(1, 1)
            with act.Fori(1, G // 2 - 1) as two:
                group(two * 2, 0)
                group(two * 2 + 1, 1)
            group(G - 2, 0)
            group(G - 1, 1, final=True)

        @block.vector
        def _(dve):
            nc.vector.memset(seed[:, :, :], 0.0).then_inc(seed_clear, 1)
            nc.vector.memset(fb_state[:, :, :], 0.0).then_inc(seed_clear, 1)
            dve.wait_ge(AB_turned, 1)
            nc.vector.tensor_copy(AT[:, :], ps_mats[0][:, 0:P])
            nc.vector.tensor_copy(BT[:, :, :].rearrange("p k n -> p (k n)"), ps_mats[0][:, P:(KT + 1) * P]).then_inc(AB_done, 1)
            UN = 2.0 ** -WTOP / XS
            HS = 2.0 ** 15 / (DM * DM * 4)
            WEIGHTS = [
                (0, wg[:, :, :, :].rearrange("p e k i -> p (e k i)"), wg16[:, :, :, :, :].rearrange("p a e k i -> p a (e k i)")),
                (1, wu[:, :, :, :].rearrange("p e k i -> p (e k i)"), wu16[:, :, :, :, :].rearrange("p a e k i -> p a (e k i)")),
                (2, rwT[:, :, :].rearrange("p k e -> p (k e)"), rw16[:, :, :, :].rearrange("p a k e -> p a (k e)")),
                (3, wd[:, :, :].rearrange("p e d -> p (e d)"), wd16[:, :, :, :].rearrange("p a e d -> p a (e d)"))]

            def greatest(i):
                nc.vector.tensor_reduce(wmax[:, i:i + 1], WEIGHTS[i][1], AX_X, ALU.max,
                                        apply_absolute_value=True).then_inc(wmax_part, 1)

            def scales():
                dve.wait_ge(wmax_known, 1)
                nc.vector.tensor_scalar(wpow[:, :], wmax_all[:, :], 2.0 ** -60, None, ALU.max).then_inc(wstep, 1)
                dve.wait_ge(wstep, 1)
                nc.vector.tensor_scalar(wpow[:, :].bitcast(I32), wpow[:, :].bitcast(I32), 0x7F800000, None,
                                        ALU.bitwise_and).then_inc(wstep, 1)
                dve.wait_ge(wstep, 2)
                nc.vector.tensor_scalar(wscale[:, :].bitcast(I32), wpow[:, :].bitcast(I32), -1.0,
                                        float((2 * 127 + WTOP) << 23), ALU.mult, ALU.add).then_inc(wstep, 1)
                nc.vector.tensor_scalar(g_un[:, :], wpow[:, 0:1], UN, None, ALU.mult).then_inc(wstep, 1)
                nc.vector.tensor_scalar(l_un[:, :], wpow[:, 2:3], 0.5 * UN, None, ALU.mult).then_inc(wstep, 1)
                nc.vector.tensor_scalar(y_un[:, 1:2], wpow[:, 3:4], wpow[:, 0:1], 2.0 ** -WTOP / HS, ALU.mult, ALU.mult).then_inc(wstep, 1)
                dve.wait_ge(wstep, 6)
                nc.vector.tensor_scalar(u_un[:, 0:1], wscale[:, 0:1], 2.0 ** -WTOP * UN * HS, None, ALU.mult).then_inc(wstep, 1)
                nc.vector.tensor_scalar(u_un[:, 1:2], wscale[:, 0:1], 2.0 ** -WTOP * UN * HS / CS, None, ALU.mult).then_inc(wstep, 1)
                nc.vector.tensor_scalar(y_un[:, 0:1], y_un[:, 1:2], wpow[:, 1:2], None, ALU.mult).then_inc(wstep, 1)
                dve.wait_ge(wstep, 9)

            def split(i):
                _, flat, parts = WEIGHTS[i]
                nc.vector.tensor_scalar(parts[:, 0, :], flat, wscale[:, i:i + 1], None, ALU.mult).then_inc(w_high[i], 1)
                dve.wait_ge(w_high[i], 1)
                nc.vector.scalar_tensor_tensor(parts[:, 1, :], flat, wscale[:, i:i + 1], parts[:, 0, :],
                                               ALU.mult, ALU.subtract).then_inc(weights_ready, 1)

            for n in range(FIRST):
                for k in range(KT):
                    dve.wait_ge(xT_turned, 2 * n + k + 1)
                    nc.vector.tensor_copy(xT[:, k, pairs[n] * 2:pairs[n] * 2 + 2, :].rearrange("p j c -> p (j c)"),
                                          ps_xT[2 * n + k][:, 0:2 * P]).then_inc(xT_first, 1)
            dve.wait_ge(Cr_turned, 1)
            nc.vector.tensor_copy(rwT[:, :, :].rearrange("p k n -> p (k n)"),
                                  ps_mats[1][:, KT * P:KT * P + KT * E]).then_inc(Cr_done, 1)
            nc.vector.tensor_copy(CT[:, :, :].rearrange("p k n -> p (k n)"),
                                  ps_mats[1][:, 0:KT * P]).then_inc(Cr_done, 1)
            dve.wait_ge(Cr_done, 1)
            greatest(2)
            for i in (0, 1, 3):
                dve.wait_ge(w_in[min(i, 2)], 16 * 2)
                greatest(i)
            scales()
            for i in (0, 1, 3, 2):
                split(i)

            def stats(k, g, src, st_sem, mv_sem, t0, t1):
                for t in range(t0, t1):
                    nc.vector.bn_stats(st[:, k, t, :], src(t)).then_inc(st_sem, 1)
                dve.wait_ge(st_sem, g * T4 + t1)
                nc.vector.memset(carrier[:, :], 0.0)
                for t in range(t0, t1):
                    nc.vector.bn_aggr(mv[:, k, t, :], st[:, k, t, :]).then_inc(mv_sem, 1)

            def piece(e, g, par, sems):
                if e in (1, 2):
                    e -= 1
                    dve.wait_ge(sems["c_done"], g * T4 + 2 * (e + 1))
                    nc.vector.tensor_tensor(y1[:, 2 * e:2 * e + 2, :], ps_misc[:, :].rearrange("p (j d) -> p j d", j=2),
                                            xskip[:, bass.ds(g * T4 + 2 * e, 2), :], ALU.add).then_inc(sems["y1_done"], 1)
                    dve.wait_ge(sems["y1_done"], g * 2 + (e + 1))
                    stats(0, g, lambda t: y1[:, t, :], sems["st1_done"], sems["mv1_done"], 2 * e, 2 * e + 2)
                elif e == 3:
                    dve.wait_ge(sems["mv1_done"], (g + 1) * T4)
                    for t in range(T4):
                        nc.vector.scalar_tensor_tensor(y1[:, t, :], y1[:, t, :], mv[:, 0, t, 0:1], gamma_bc[:, :],
                                                       ALU.subtract, ALU.mult).then_inc(sems["scaled1"], 1)
                    dve.wait_ge(sems["rstd1_ready"], g + 1)
                    for t in range(T4):
                        dve.wait_ge(sems["scaled1"], g * T4 + (t + 1))
                        nc.vector.scalar_tensor_tensor(y1[:, t, :], y1[:, t, :], rstd[:, 0, 1, t:t + 1],
                                                       xres[:, g * T4 + t, :], ALU.mult, ALU.add).then_inc(sems["z1_done"], 1)
                elif e == 4:
                    dve.wait_ge(sems["z1_done"], (g + 1) * T4)
                    stats(1, g, lambda t: y1[:, t, :], sems["st2_done"], sems["mv2_done"], 0, T4)
                elif e == 5:
                    dve.wait_ge(sems["rstd2_ready"], g + 1)
                    dve.wait_ge(sems["mv2_done"], (g + 1) * T4)
                    for t in range(T4):
                        nc.vector.tensor_scalar(x2[:, par, t, :], y1[:, t, :], mv[:, 1, t, 0:1],
                                                rstd[:, 1, 1, t:t + 1], ALU.subtract, ALU.mult).then_inc(sems["x2_ready"], 1)
                elif e in (6, 7):
                    half = e - 6
                    dve.wait_ge(sems["x2_high"], g * 2 + half + 1)
                    nc.vector.scalar_tensor_tensor(
                        x2T[:, par, 1, :, half * 2 * P:(half + 1) * 2 * P],
                        ps_misc[:, :].rearrange("p (k t) -> p k t", k=KT), XS,
                        x2T[:, par, 0, :, half * 2 * P:(half + 1) * 2 * P], ALU.mult, ALU.subtract).then_inc(sems["x2_low"], 1)

            tt, ts = nc.vector.tensor_tensor, nc.vector.tensor_scalar

            def choose(g, sems):
                done = 0

                def then(ins):
                    nonlocal done
                    done += 1
                    ins.then_inc(sems["choice_step"], 1)
                    dve.wait_ge(sems["choice_step"], g * CHOICE_STEPS + done)

                dve.wait_ge(sems["th_done"], g + 1)
                then(ts(score[:, :, :], th[:, :, :], 0.5, 0.5, ALU.mult, ALU.add))
                then(tt(choice[:, :, :], score[:, :, :], cbias_bc[:, :].unsqueeze(1).to_broadcast([P, T4, E]), ALU.add))
                by2 = choice[:, :, :].rearrange("p t (q a) -> p t q a", a=2)
                tt(more[:, :, :], by2[:, :, :, 0], by2[:, :, :, 1], ALU.max)
                then(tt(both[:, :, :], by2[:, :, :, 0], by2[:, :, :, 1], ALU.add))
                more2 = more[:, :, :].rearrange("p t (q a) -> p t q a", a=2)
                both2 = both[:, :, :].rearrange("p t (q a) -> p t q a", a=2)
                tt(top[:, :, :], both2[:, :, :, 0], both2[:, :, :, 1], ALU.max)
                then(tt(across[:, :, :], more2[:, :, :, 0], more2[:, :, :, 1], ALU.add))
                then(tt(top[:, :, :], top[:, :, :], across[:, :, :], ALU.max))
                tt(mask[:, :, 0:1], top[:, :, 0:1], top[:, :, 1:2], ALU.is_ge)
                then(tt(mask[:, :, 1:2], top[:, :, 0:1], top[:, :, 1:2], ALU.is_lt))
                by_group = choice[:, :, :].rearrange("p t (q a) -> p t q a", q=2)
                then(tt(by_group, by_group, mask[:, :, :].unsqueeze(3).to_broadcast([P, T4, 2, EPG]), ALU.mult))
                of_j = choice[:, :, :].unsqueeze(2).to_broadcast([P, T4, E, E])
                of_i = choice[:, :, :].unsqueeze(3).to_broadcast([P, T4, E, E])
                tt(ahead[:, :, :, :], of_j, of_i, ALU.is_gt)
                then(tt(level[:, :, :, :], of_j, of_i, ALU.is_equal))
                then(tt(level[:, :, :, :], level[:, :, :, :], lower[:, :, :].unsqueeze(1).to_broadcast([P, T4, E, E]), ALU.mult))
                then(tt(ahead[:, :, :, :], ahead[:, :, :, :], level[:, :, :, :], ALU.add))
                assert done == CHOICE_STEPS, done

            def weigh(g):
                done = 0

                def then(ins):
                    nonlocal done
                    done += 1
                    ins.then_inc(route_step, 1)
                    dve.wait_ge(route_step, g * STEPS + done)

                then(nc.vector.tensor_reduce(rank[:, :, :], ahead[:, :, :, :], AX_X, ALU.add))
                flat = [v[:, :, :].rearrange("p t e -> p (t e)") for v in (kept, rank, score)]
                then(nc.vector.scalar_tensor_tensor(flat[0], flat[1], 2.0, flat[2], ALU.is_lt, ALU.mult))
                then(nc.vector.tensor_reduce(total[:, :, 0], kept[:, :, :], AX_X, ALU.add))
                then(ts(total[:, :, 1], total[:, :, 0], 1e-20, 1.0 / CS, ALU.add, ALU.mult))
                then(nc.vector.reciprocal(total[:, :, 0], total[:, :, 1]))
                then(tt(kept[:, :, :], kept[:, :, :], total[:, :, 0:1].to_broadcast([P, T4, E]), ALU.mult))
                if not isinstance(g, int) or g:
                    dve.wait_ge(comb_turned, g)
                then(nc.vector.tensor_copy(comb[:, :, 0, :], kept[:, :, :]))
                then(tt(comb[:, :, 1, :], kept[:, :, :], comb[:, :, 0, :], ALU.subtract))
                assert done == STEPS, done

            dve.wait_ge(res_done, 2)
            dve.wait_ge(weights_ready, 4)
            for e in range(E1):
                piece(e, 0, 0, main)
            choose(0, main)

            dve.wait_ge(scan_tanh, WARM + 2 * L)
            nc.vector.tensor_tensor(met_diff[:, :, :],
                                    states[:, L - 1, :].rearrange("p (b c) -> p b c", b=NB)[:, :, 0:NCH - 1],
                                    seed[:, :, 1:NCH], ALU.subtract).then_inc(met_step, 1)
            dve.wait_ge(met_step, 1)
            nc.vector.tensor_reduce(met_row[:, 0:1], met_diff[:, :, :].rearrange("p b c -> p (b c)"), AX_X, ALU.max,
                                    apply_absolute_value=True).then_inc(met_part, 1)
            dve.wait_ge(met_all, 1)
            nc.vector.tensor_scalar(met[:, :], met_row[:, 1:2], MET, None, ALU.is_le).then_inc(met_known, 1)
            dve.wait_ge(met_known, 1)
            runs_met = dve.value_load(met[0:1, 0:1], min_val=0, max_val=1)
            with dve.If(runs_met == 0):
                for e in range(E1):
                    piece(e, 0, 0, again)
                choose(0, again)

            def inner(g, e, b):
                n = g * E1 + e
                dve.wait_ge(silu_done, n + 1)
                if not isinstance(n, int) or n >= 2:
                    dve.wait_ge(h_low, n - 1)
                if e == 0:
                    nc.vector.scalar_tensor_tensor(h[:, b, :], ps_u[b][:, :], u_un[:, 0:1], sg[:, b, :],
                                                   ALU.mult, ALU.mult).then_inc(gu_done, 1)
                else:
                    nc.vector.scalar_tensor_tensor(gu[:, b, :], ps_u[b][:, :], u_un[:, 1:2], sg[:, b, :],
                                                   ALU.mult, ALU.mult).then_inc(gu_done, 1)
                    dve.wait_ge(gu_done, n + 1)
                    dve.wait_ge(cb_done, g * E + e)
                    nc.vector.tensor_tensor(h[:, b, :], ps_comb[:, :], gu[:, b, :], ALU.mult).then_inc(h_done, 1)

            def close(step, g, par):
                if step == 0:
                    dve.wait_ge(down_done, (g + 1) * E1)
                    for j in range(2):
                        part = x2[:, par, 2 * j:2 * j + 2, :]
                        nc.vector.scalar_tensor_tensor(part, ps_y[j][:, :].rearrange("p (j d) -> p j d", j=2), y_un[:, 0:1],
                                                       part, ALU.mult, ALU.add).then_inc(z2_done, 1)
                elif step == 1:
                    dve.wait_ge(z2_done, (g + 1) * 2)
                    stats(2, g, lambda t: x2[:, par, t, :], st3_done, mv3_done, 0, T4)
                else:
                    dve.wait_ge(rstd3_ready, g + 1)
                    dve.wait_ge(mv3_done, (g + 1) * T4)
                    for t in range(T4):
                        nc.vector.tensor_scalar(xskip[:, g * T4 + t, :], x2[:, par, t, :], mv[:, 2, t, 0:1],
                                                rstd[:, 2, 1, t:t + 1], ALU.subtract, ALU.mult).then_inc(out_ready, 1)

            def group(g, par, first=False, final=False):
                for e in range(E1):
                    inner(g, e, (par + e) % 2)
                    if e in (1, 2, 3) and not first:
                        close(e - 1, g - 1, 1 - par)
                    if not final:
                        piece(e, g + 1, 1 - par, main)
                        if e == E1 - 1:
                            choose(g + 1, main)
                            weigh(g + 1)

            weigh(0)
            dve.wait_ge(res_done, L // T4)
            group(0, 0, first=True)
            group(1, 1)
            with dve.Fori(1, G // 2 - 1) as two:
                group(two * 2, 0)
                group(two * 2 + 1, 1)
            group(G - 2, 0)
            group(G - 1, 1, final=True)
            close(0, G - 1, 1)
            close(1, G - 1, 1)
            close(2, G - 1, 1)

        @block.gpsimd
        def _(pool):
            nc.gpsimd.memset(ident[:, :], 0.0).then_inc(const_step, 1)
            pool.wait_ge(const_step, 1)
            nc.gpsimd.affine_select(out=ident[:, :], in_=ident[:, :], compare_op=ALU.not_equal, fill=1.0, base=0,
                                    pattern=[[-1, P]], channel_multiplier=1).then_inc(consts, 1)
            pool.wait_ge(consts, 1)
            nc.gpsimd.tensor_copy(ident16[:, :], ident[:, :]).then_inc(consts, 1)
            nc.gpsimd.memset(pick[:, :, :], 0.0).then_inc(const_step, 1)
            pool.wait_ge(const_step, 2)
            for a in range(2):
                nc.gpsimd.affine_select(out=pick[:, :, :], in_=pick[:, :, :], compare_op=ALU.not_equal, fill=1.0,
                                        base=-a * E, pattern=[[-1, E], [0, P]], channel_multiplier=1).then_inc(const_step, 1)
                pool.wait_ge(const_step, 3 + a)
            nc.gpsimd.memset(lower[:, :, :], 1.0).then_inc(const_step, 1)
            pool.wait_ge(const_step, 5)
            nc.gpsimd.affine_select(out=lower[:, :, :], in_=lower[:, :, :], compare_op=ALU.is_gt, fill=0.0, base=0,
                                    pattern=[[1, E], [-1, E]], channel_multiplier=0)
            nc.gpsimd.memset(eps[:, :], LN_EPS)
            nc.gpsimd.memset(neghalf[:, :], -0.5).then_inc(const_step, 1)
            pool.wait_ge(const_step, 6)
            pool.wait_ge(vecs_in, 16 * NVEC)
            nc.gpsimd.tensor_scalar(D_bc[:, :], D_bc[:, :], 1.0, None, ALU.add).then_inc(const_step, 1)
            pool.wait_ge(const_step, 7)

            def skip(n):
                c = chunks[n]
                pool.wait_ge(x_in[c], 16)
                nc.gpsimd.tensor_tensor(xskip[:, c * T4:(c + 1) * T4, :], xres[:, c * T4:(c + 1) * T4, :],
                                        D_bc[:, :].unsqueeze(1).to_broadcast([P, T4, DM]), ALU.mult).then_inc(skip_done, 1)

            def residual(n):
                c = chunks[n]
                pool.wait_ge(skip_done, n + 1)
                pool.wait_ge(xT_turned, T4 * (n + 1))
                nc.gpsimd.tensor_tensor(xres[:, c * T4:(c + 1) * T4, :], xres[:, c * T4:(c + 1) * T4, :],
                                        beta_bc[:, :].unsqueeze(1).to_broadcast([P, T4, DM]), ALU.add).then_inc(res_done, 1)

            for n in range(L // T4):
                skip(n)
                if n == 3:
                    pool.wait_ge(wmax_part, 4)
                    nc.gpsimd.partition_all_reduce(wmax_all[:, :], wmax[:, :], P, RMAX).then_inc(wmax_known, 1)
                residual(n)

            def copy_states(g):
                if not isinstance(g, int) or g > 1:
                    pool.wait_ge(main["c_done"], g * T4)
                nc.gpsimd.tensor_copy(gstates[:, :, :], states[:, bass.ds(g * T4, T4), :]).then_inc(gstates_ready, 1)

            def rsqrt(k, g, mv_sem, step_sem, ready, count):
                pool.wait_ge(mv_sem, (g + 1) * T4)
                nc.gpsimd.tensor_tensor(rstd[:, k, 0, :], mv[:, k, :, 1], eps[:, :], ALU.add).then_inc(step_sem, 1)
                pool.wait_ge(step_sem, count + 1)
                nc.gpsimd.tensor_tensor(rstd[:, k, 1, :], rstd[:, k, 0, :], neghalf[:, :], ALU.pow).then_inc(ready, 1)

            rsqrt(0, 0, main["mv1_done"], rstd_step, main["rstd1_ready"], 0)
            rsqrt(1, 0, main["mv2_done"], rstd_step, main["rstd2_ready"], 1)
            pool.wait_ge(met_part, 1)
            nc.gpsimd.partition_all_reduce(met_row[:, 1:2], met_row[:, 0:1], P, RMAX).then_inc(met_all, 1)
            pool.wait_ge(met_known, 1)
            runs_met = pool.value_load(met[0:1, 0:1], min_val=0, max_val=1)
            with pool.If(runs_met == 0):
                rsqrt(0, 0, again["mv1_done"], again_rstd_step, again["rstd1_ready"], 0)
                rsqrt(1, 0, again["mv2_done"], again_rstd_step, again["rstd2_ready"], 1)

            def low(g, e, b):
                pool.wait_ge(h_high, g * E1 + (e + 1))
                nc.gpsimd.tensor_tensor(h16[:, e % 3, 1, :], h[:, b, :], h16[:, e % 3, 0, :], ALU.subtract).then_inc(h_low, 1)

            pool.wait_ge(runs_done, 1)

            def group(g, par, first=False, final=False):
                count = g * 3 + (2 if first else 1)
                if not final:
                    copy_states(g + 1)
                for e in range(E1):
                    low(g, e, (par + e) % 2)
                    if e == 2 and not first:
                        rsqrt(2, g - 1, mv3_done, rstd_step, rstd3_ready, count)
                    if e == 2 and not final:
                        rsqrt(0, g + 1, main["mv1_done"], rstd_step, main["rstd1_ready"], count + (0 if first else 1))
                    elif e == 4 and not final:
                        rsqrt(1, g + 1, main["mv2_done"], rstd_step, main["rstd2_ready"], count + (1 if first else 2))

            group(0, 0, first=True)
            group(1, 1)
            with pool.Fori(1, G // 2 - 1) as two:
                group(two * 2, 0)
                group(two * 2 + 1, 1)
            group(G - 2, 0)
            group(G - 1, 1, final=True)
            rsqrt(2, G - 1, mv3_done, rstd_step, rstd3_ready, (G - 1) * 3 + 2)


_INS = ["L0_attn_x", "L0_attn_A", "L0_attn_B", "L0_attn_C", "L0_attn_D", "L0_attn_gamma", "L0_attn_beta",
        "L0_ffn_router_weight", "L0_ffn_correction_bias", "L0_ffn_w_gate", "L0_ffn_w_up", "L0_ffn_w_down",
        "L0_ffn_sw_gate", "L0_ffn_sw_up", "L0_ffn_sw_down"]


def kernel(**inputs):
    import numpy as np
    import concourse.bacc as bacc
    from concourse.bass_utils import run_bass_kernel_spmd

    nc = bacc.Bacc("TRN2", target_bir_lowering=False, num_devices=1)
    arrays, args = {}, []
    for name in _INS:
        a = np.ascontiguousarray(inputs[name])
        arrays[f"in_{name}_dram"] = a
        args.append(nc.dram_tensor(f"in_{name}_dram", a.shape, mybir.dt.from_np(a.dtype), kind="ExternalInput").ap())
    shape = inputs["L0_attn_x"].shape
    args.append(nc.dram_tensor("out_0_dram", shape, F32, kind="ExternalOutput").ap())
    ssm_moe_kernel(nc, *args)
    r = run_bass_kernel_spmd(nc, [arrays], core_ids=[0])
    return r.results[0]["out_0_dram"]
```

```python
from contextlib import ExitStack

import concourse.bass as bass
from concourse import mybir

ALU = mybir.AluOpType
ACT = mybir.ActivationFunctionType
F32 = mybir.dt.float32
F16 = mybir.dt.float16
I32 = mybir.dt.int32
AX_X = mybir.AxisListType.X
RMAX = bass.bass_isa.ReduceOp.max
P = 128

LN_EPS = 1e-5
MET = 2.0 ** -20


def ssm_moe_kernel(nc, x, A, B, C, D, gamma, beta, router_weight, correction_bias,
                   w_gate, w_up, w_down, sw_gate, sw_up, sw_down, comb_dram, out):
    NB, S, DM = x.shape
    NS = A.shape[0]
    E, _, I = w_gate.shape
    KT = DM // P
    L = NB * S // P
    NCH = P // NB
    WARM = 4
    T4 = 4
    G = L // T4
    GT = T4 * P
    E1 = E + 1
    EPG = E // 2
    assert NS == P and I == P and DM == 2 * P and G == 8 and E == 8

    XS = 2.0 ** 11
    WTOP = 14

    with ExitStack() as ctx:
        def sb(name, shape, dt=F32):
            return ctx.enter_context(nc.sbuf_tensor(name, shape, dt))

        def sem(name):
            return ctx.enter_context(nc.semaphore(name))

        xres = sb("xres", [P, L, DM])
        xskip = sb("xskip", [P, L, DM])
        xT = sb("xT", [P, KT, L, P])
        states = sb("states", [P, L, P])
        run_state = sb("run_state", [P, 2, P])
        seed = sb("seed", [P, NB, NCH])
        fb_state = sb("fb_state", [P, 2, NB])
        met_diff = sb("met_diff", [P, NB, NCH - 1])
        met_row = sb("met_row", [P, 2])
        met = sb("met", [P, 1], I32)
        act_warm = sb("act_warm", [P, 1])

        ident = sb("ident", [P, P])
        A_sb = sb("A_sb", [P, NS])
        B_sb = sb("B_sb", [P, DM])
        C_sb = sb("C_sb", [P, KT, NS])
        rw_sb = sb("rw_sb", [E, DM])
        AT = sb("AT", [P, NS])
        BT = sb("BT", [P, KT, NS])
        CT = sb("CT", [P, KT, P])
        C16 = sb("C16", [P, 2, KT, P], F16)
        rwT = sb("rwT", [P, KT, E])
        rw16 = sb("rw16", [P, 2, KT, E], F16)
        D_bc = sb("D_bc", [P, DM])
        gamma_bc = sb("gamma_bc", [P, DM])
        beta_bc = sb("beta_bc", [P, DM])
        cbias_bc = sb("cbias_bc", [P, E])

        wg = sb("wg", [P, E1, KT, I])
        wu = sb("wu", [P, E1, KT, I])
        wd = sb("wd", [P, E1, DM])
        wg16 = sb("wg16", [P, 2, E1, KT, I], F16)
        wu16 = sb("wu16", [P, 2, E1, KT, I], F16)
        wd16 = sb("wd16", [P, 2, E1, DM], F16)
        wmax = sb("wmax", [P, 5])
        wmax_all = sb("wmax_all", [P, 5])
        wpow = sb("wpow", [P, 5])
        wscale = sb("wscale", [P, 5])
        g_un = sb("g_un", [P, 1])
        u_un = sb("u_un", [P, 1])
        c_un = sb("c_un", [P, 1])
        l_un = sb("l_un", [P, 1])
        y_un = sb("y_un", [P, 2])

        late = xT[:, :, :, :].rearrange("p k l c -> p (k l c)")
        sg, gu, h = (late[:, i * 2 * GT:(i + 1) * 2 * GT].rearrange("p (b t) -> p b t", b=2) for i in range(3))
        states16 = late[:, 6 * GT:7 * GT].bitcast(F16).rearrange("p (a t c) -> p a t c", a=2, t=T4)
        comb_all = late[:, 7 * GT:(7 + E) * GT].rearrange("p (e t) -> p e t", e=E)
        x2 = wg[:, :, :, :].rearrange("p e k i -> p (e k i)")[:, 0:2 * T4 * DM].rearrange("p (a t d) -> p a t d", a=2, t=T4)
        y1 = wu[:, :, :, :].rearrange("p e k i -> p (e k i)")[:, 0:T4 * DM].rearrange("p (t d) -> p t d", t=T4)
        z2 = wd[:, :, :].rearrange("p e d -> p (e d)")[:, 0:T4 * DM].rearrange("p (t d) -> p t d", t=T4)
        st = sb("st", [P, 3, T4, 6])
        mv = sb("mv", [P, 3, T4, 2])
        rstd = sb("rstd", [P, 3, 2, T4])
        neghalf = sb("neghalf", [P, T4])
        carrier = sb("carrier", [P, 1])
        eps = sb("eps", [P, T4])
        x2T = sb("x2T", [P, 2, 2, KT, GT], F16)
        th = sb("th", [P, T4, E])
        score = sb("score", [P, T4, E])
        choice = sb("choice", [P, T4, E])
        more, both = sb("more", [P, T4, E // 2]), sb("both", [P, T4, E // 2])
        top, across, mask, total = (sb(n, [P, T4, 2]) for n in ("top", "across", "mask", "total"))
        ahead, level = sb("ahead", [P, T4, E, E]), sb("level", [P, T4, E, E])
        lower = sb("lower", [P, E, E])
        rank, kept = sb("rank", [P, T4, E]), sb("kept", [P, T4, E])
        h16 = sb("h16", [P, 3, 2, GT], F16)
        comb = sb("comb", [P, T4, E])
        combT = sb("combT", [E, GT])

        bank = [ctx.enter_context(nc.psum_tensor(f"bank{i}", [P, 512], F32)) for i in range(8)]
        ps_scan = bank[4:6]
        ps_xT, ps_mats = bank[0:4], bank[6:8]
        ps_g, ps_u, ps_y = bank[0:2], bank[2:4], bank[4:6]
        ps_comb, ps_misc = bank[6], bank[7]

        x_in = [sem(f"x_in{i}") for i in range(L // T4)]
        x_rest = sem("x_rest")
        AB_in, Cr_in, D_in, vecs_in = sem("AB_in"), sem("Cr_in"), sem("D_in"), sem("vecs_in")
        w_in = [sem(f"w_in{i}") for i in range(3)]
        const_step, consts = sem("const_step"), sem("consts")
        AB_turned, AB_done, Cr_turned, Cr_done = sem("AB_turned"), sem("AB_done"), sem("Cr_turned"), sem("Cr_done")
        xT_turned, xT_first, xT_done = sem("xT_turned"), sem("xT_first"), sem("xT_done")
        seed_clear, scan_mm, scan_tanh = sem("seed_clear"), sem("scan_mm"), sem("scan_tanh")
        met_step, met_part, met_all, met_known = sem("met_step"), sem("met_part"), sem("met_all"), sem("met_known")
        fb_mm, fb_tanh, fb_kept = sem("fb_mm"), sem("fb_tanh"), sem("fb_kept")
        skip_done, res_done = sem("skip_done"), sem("res_done")
        wmax_part, wmax_known, wstep, weights_ready = sem("wmax_part"), sem("wmax_known"), sem("wstep"), sem("weights_ready")
        w_high = [sem(f"w_high{i}") for i in range(5)]

        def ahead_sems(prefix):
            names = ("c_done y1_done st1_done mv1_done scaled1 z1_done st2_done mv2_done x2_ready "
                     "rstd1_ready rstd2_ready x2_turned x2_high x2_low logits_done th_done choice_step route_step").split()
            return {name: sem(prefix + name) for name in names}

        main, again = ahead_sems(""), ahead_sems("again_")
        again_up, again_rstd_step = sem("again_up"), sem("again_rstd_step")
        states_high, states_low, rstd_step, rstd3_ready = sem("states_high"), sem("states_low"), sem("rstd_step"), sem("rstd3_ready")
        comb_turned, combT_ready, comb_written = sem("comb_turned"), sem("combT_ready"), sem("comb_written")
        comb_in = [sem(f"comb_in{e}") for e in range(E)]
        up_done, silu_done, gu_done, h_done, h_high, h_low, down_done = (
            sem("up_done"), sem("silu_done"), sem("gu_done"), sem("h_done"),
            sem("h_high"), sem("h_low"), sem("down_done"))
        last_down = sem("last_down")
        z2_done, st3_done, mv3_done, out_ready, out_sent = (
            sem("z2_done"), sem("st3_done"), sem("mv3_done"), sem("out_ready"), sem("out_sent"))

        x_dram = x.rearrange("b s d -> (b s) d").rearrange("(p l) d -> p l d", l=L)
        out_dram = out.rearrange("b s d -> (b s) d").rearrange("(p l) d -> p l d", l=L)

        chunks = [L // T4 - 1] + list(range(L // T4 - 1))
        pairs = [c * T4 // 2 + j for c in chunks for j in range(T4 // 2)]
        WEIGHT_LOADS = [
            (w_gate.rearrange("e (k p) i -> p (e k) i", p=P), wg[:, 1:E1, :, :].rearrange("p e k i -> p (e k) i"),
             sw_gate.rearrange("(k p) i -> p k i", p=P), wg[:, 0, :, :]),
            (w_up.rearrange("e (k p) i -> p (e k) i", p=P), wu[:, 1:E1, :, :].rearrange("p e k i -> p (e k) i"),
             sw_up.rearrange("(k p) i -> p k i", p=P), wu[:, 0, :, :]),
            (w_down.rearrange("e i d -> i e d"), wd[:, 1:E1, :], sw_down, wd[:, 0, :])]
        NVEC = 3
        FIRST = 2
        HALVES = 2 * (len(pairs) - FIRST)
        PE_AT = {1: (0, 0), 2: (0, 1), 4: (1, 0), 5: (1, 1), 16: (4, 0), 17: (4, 1), 20: (5, 0), 21: (5, 1),
                 24: (6, 0), 25: (6, 1)}
        ACT_AT = {18: 5, 22: 6, 26: 7}
        UP_FROM = 26
        WHOLE = 2
        NUP = 2 * 3 * KT
        CHOICE_STEPS, STEPS = 10, 6

        block = ctx.enter_context(nc.Block())

        @block.sync
        def _(sp):
            def load_x(n):
                parts = [(0, 2, x_in[chunks[n]]), (2, 4, x_rest)] if n == 0 else [(0, 4, x_in[chunks[n]])]
                for t0, t1, arrived in parts:
                    part = slice(chunks[n] * T4 + t0, chunks[n] * T4 + t1)
                    sp.dma_start(xres[:, part, :], x_dram[:, part, :]).then_inc(arrived, 16)

            def load_weights(i):
                routed, to_routed, shared, to_shared = WEIGHT_LOADS[i]
                sp.dma_start(to_routed, routed).then_inc(w_in[i], 16)
                sp.dma_start(to_shared, shared).then_inc(w_in[i], 16)

            sp.dma_start(A_sb[:, :], A).then_inc(AB_in, 16)
            sp.dma_start(B_sb[:, :], B).then_inc(AB_in, 16)
            load_x(0)
            load_x(1)
            sp.dma_start(C_sb[:, :, :], C.rearrange("(k p) n -> p k n", p=P)).then_inc(Cr_in, 16)
            sp.dma_start(rw_sb[:, :], router_weight).then_inc(Cr_in, 16)
            sp.dma_start(D_bc[:, :], D.partition_broadcast(P)).then_inc(D_in, 16)
            load_x(2)
            load_weights(0)
            load_x(3)
            load_x(4)
            load_weights(1)
            load_x(5)
            load_weights(2)
            load_x(6)
            sp.dma_start(gamma_bc[:, :], gamma.partition_broadcast(P)).then_inc(vecs_in, 16)
            sp.dma_start(beta_bc[:, :], beta.partition_broadcast(P)).then_inc(vecs_in, 16)
            sp.dma_start(cbias_bc[:, :], correction_bias.partition_broadcast(P)).then_inc(vecs_in, 16)
            load_x(7)

            def send(tile, count):
                sp.wait_ge(out_ready, tile + count)
                sp.dma_start(out_dram[:, bass.ds(tile, count), :], xskip[:, bass.ds(tile, count), :]).then_inc(out_sent, 16)

            def spread_comb(g):
                sp.wait_ge(combT_ready, g + 1)
                there = comb_dram[:, bass.ds(g * GT, GT)]
                sp.dma_start(there, combT[:, :]).then_inc(comb_written, 16)
                sp.wait_ge(comb_written, (g + 1) * 16)
                for e in range(E):
                    if not isinstance(g, int):
                        sp.wait_ge(h_done, (g - 1) * E + (e + 1))
                    sp.dma_start(comb_all[:, e, :], comb_dram[e, bass.ds(g * GT, GT)].partition_broadcast(P)
                                 ).then_inc(comb_in[e], 16)

            spread_comb(0)
            with sp.Fori(1, G) as g:
                spread_comb(g)
                send((g - 1) * T4, T4)
            send(L - 4, 2)
            send(L - 2, 2)
            sp.wait_ge(out_sent, 16 * (G + 1))

        @block.tensor
        def _(pe):
            pe.wait_ge(consts, 1)
            pe.wait_ge(AB_in, 16 * 2)
            pe.transpose(ps_mats[0][:, 0:P], A_sb[:, :], ident[:, :])
            for k in range(KT):
                last = pe.transpose(ps_mats[0][:, (k + 1) * P:(k + 2) * P], B_sb[:, k * P:(k + 1) * P], ident[:, :])
            last.then_inc(AB_turned, 1)

            def turn_Cr():
                pe.wait_ge(Cr_in, 16 * 2)
                for k in range(KT):
                    pe.transpose(ps_mats[1][:, k * P:(k + 1) * P], C_sb[:, k, :], ident[:, :])
                for k in range(KT):
                    last = pe.transpose(ps_mats[1][:, KT * P + k * E:KT * P + (k + 1) * E], rw_sb[:, k * P:(k + 1) * P],
                                        ident[0:E, 0:E])
                last.then_inc(Cr_turned, 1)

            def turn_x(n, k):
                pair = pairs[n]
                pe.wait_ge(x_rest if n == 1 else x_in[pair * 2 // T4], 16)
                for j in range(2):
                    last = pe.transpose(ps_xT[(2 * n + k) % 4][:, j * P:(j + 1) * P],
                                        xres[:, pair * 2 + j, k * P:(k + 1) * P], ident[:, :])
                last.then_inc(xT_turned, 1)

            def drive(s, tile):
                if s % 2 == 0 and s < 2 * FIRST:
                    pe.wait_ge(xT_first, s + 2)
                elif s % 2 == 0 and s < L:
                    pe.wait_ge(xT_done, s - 2 * FIRST + 2)
                for k in range(KT):
                    pe.matmul(ps_scan[s % 2][:, 0:P], BT[:, k, :], xT[:, k, tile, :], start=(k == 0), stop=False)

            def scan_step(s, tiles, before):
                if s:
                    pe.wait_ge(scan_tanh, s)
                pe.matmul(ps_scan[s % 2][:, 0:P], AT[:, :], before, start=False, stop=True).then_inc(scan_mm, 1)
                if s + 1 < len(tiles):
                    drive(s + 1, tiles[s + 1])

            for n in range(FIRST):
                for k in range(KT):
                    turn_x(n, k)
            pe.wait_ge(AB_done, 1)
            pe.wait_ge(seed_clear, 2)
            seeds = seed[:, :, :].rearrange("p b c -> p (b c)")
            tiles = list(range(L - WARM, L)) + 2 * list(range(L))
            drive(0, tiles[0])
            for s in range(WARM + L):
                scan_step(s, tiles, seeds if s in (0, WARM) else run_state[:, (s - 1) % 2, :])
                if s < HALVES:
                    turn_x(FIRST + s // 2, s % 2)
                if s == WARM:
                    turn_Cr()

            def piece(e, g, par, sems, halves=(0, 1)):
                for half in halves:
                    if e in (0, 1):
                        if half == 0 and e == 1:
                            pe.wait_ge(sems["y1_done"], g * 2 + 1)
                        elif half == 0 and (not isinstance(g, int) or g):
                            pe.wait_ge(sems["th_done"], g)
                        elif half == 0:
                            pe.wait_ge(Cr_done, 2)
                        dst = ps_misc[:, half * DM:(half + 1) * DM]
                        t = 2 * e + half
                        if isinstance(g, int) and g < WHOLE:
                            last = pe.matmul(dst, states[:, g * T4 + t, :], CT[:, :, :].rearrange("p k d -> p (k d)"),
                                             start=True, stop=True)
                        else:
                            pe.wait_ge(states_low, g - WHOLE + 1)
                            for m, (ps, pc) in enumerate(((0, 0), (0, 1), (1, 0))):
                                last = pe.matmul(dst, states16[:, ps, t, :], C16[:, pc, :, :].rearrange("p k d -> p (k d)"),
                                                 start=(m == 0), stop=(m == 2))
                        last.then_inc(sems["c_done"], 1)
                    elif e in (4, 5):
                        if half == 0 and e == 4:
                            pe.wait_ge(sems["x2_ready"], g * T4 + 2)
                        elif half == 0:
                            pe.wait_ge(sems["x2_low"], g * 2 + 1)
                        for j in range(2):
                            pe.transpose(ps_misc[:, (half * 2 + j) * P:(half * 2 + j + 1) * P],
                                         x2[:, par, 2 * (e - 4) + j, half * P:(half + 1) * P],
                                         ident[:, :]).then_inc(sems["x2_turned"], 1)
                    elif e == 6:
                        if half == 0:
                            pe.wait_ge(sems["x2_low"], g * 2 + 2)
                        for t in (2 * half, 2 * half + 1):
                            n = 0
                            for px, pw in ((0, 0), (0, 1), (1, 0)):
                                for k in range(KT):
                                    last = pe.matmul(ps_misc[:, t * E:(t + 1) * E], x2T[:, par, px, k, t * P:(t + 1) * P],
                                                     rw16[:, pw, k, :], start=(n == 0), stop=(n == 3 * KT - 1))
                                    n += 1
                            last.then_inc(sems["logits_done"], 1)

            def up_products(e, par, b, of=range(NUP)):
                for n in of:
                    ps, w = ((ps_g[b], wg16), (ps_u[b], wu16))[n // (NUP // 2)]
                    m = n % (NUP // 2)
                    pw, px = ((0, 0), (0, 1), (1, 0))[m % 3]
                    last = pe.matmul(ps[:, :], w[:, pw, e, m // 3, :], x2T[:, par, px, m // 3, :],
                                     start=(m == 0), stop=(m == NUP // 2 - 1))
                return last

            def up(g, e, par, b):
                n = g * E1 + e
                if not isinstance(n, int) or n >= 2:
                    pe.wait_ge(gu_done, n - 1)
                if e == 0:
                    pe.wait_ge(main["x2_low"], g * 2 + 2)
                up_products(e, par, b).then_inc(up_done, 1)

            def early_up(n):
                last = up_products(n // NUP, 0, n // NUP, of=(n % NUP,))
                if n % NUP == NUP - 1:
                    last.then_inc(up_done, 1)

            n_up = 0
            for i in range(L):
                s = WARM + L + i
                scan_step(s, tiles, seeds if i == 0 else states[:, i - 1, :])
                if i in PE_AT:
                    e, half = PE_AT[i]
                    piece(e, 0, 0, main, halves=(half,))
                if i == UP_FROM:
                    pe.wait_ge(weights_ready, 5)
                if i >= UP_FROM:
                    for n in (n_up, n_up + 1):
                        early_up(n)
                    n_up += 2
            for n in range(n_up, 2 * NUP):
                early_up(n)

            pe.wait_ge(met_known, 1)
            runs_met = pe.value_load(met[0:1, 0:1], min_val=0, max_val=1)
            with pe.If(runs_met == 0):
                with pe.Fori(0, NCH) as c:
                    with pe.Fori(0, L // 2) as l:
                        for j in range(2):
                            for k in range(KT):
                                pe.matmul(ps_scan[j][:, 0:NB], BT[:, k, :],
                                          xT[:, k, l * 2 + j, :].rearrange("p (b c) -> p c b", b=NB)[:, c, :],
                                          start=(k == 0), stop=False)
                            pe.wait_ge(fb_tanh, c * L + l * 2 + (j + 1))
                            pe.matmul(ps_scan[j][:, 0:NB], AT[:, :], fb_state[:, 1 - j, :],
                                      start=False, stop=True).then_inc(fb_mm, 1)
                pe.wait_ge(fb_kept, NCH * L)
                for e in range(E1):
                    piece(e, 0, 0, again)
                for e in range(2):
                    up_products(e, 0, e).then_inc(again_up, 1)
                pe.wait_ge(again["route_step"], STEPS)

            def turn_comb(g):
                pe.wait_ge(main["route_step"], (g + 1) * STEPS)
                if not isinstance(g, int) or g:
                    pe.wait_ge(combT_ready, g)
                for t in range(T4):
                    last = pe.transpose(ps_comb[0:E, t * P:(t + 1) * P], comb[:, t, :], ident[:, :])
                last.then_inc(comb_turned, 1)

            def down_product(e, t, m, start=False):
                ph, pw = ((0, 0), (0, 1), (1, 0))[m]
                return pe.matmul(ps_y[t // 2][:, (t % 2) * DM:(t % 2 + 1) * DM],
                                 h16[:, e % 3, ph, t * P:(t + 1) * P], wd16[:, pw, e, :],
                                 start=start, stop=(e == E1 - 1 and m == 2), skip_group_check=True)

            def down(g, e):
                pe.wait_ge(h_low, g * E1 + (e + 1))
                if e == 0 and (not isinstance(g, int) or g):
                    pe.wait_ge(z2_done, 2 * g)
                for t in range(T4):
                    for m in range(3):
                        last = down_product(e, t, m, start=(e == 0 and t % 2 == 0 and m == 0))
                last.then_inc(down_done, 1)

            def group(g, par, first=False, final=False):
                for e in range(E1):
                    b = (par + e) % 2
                    if e < E1 - 1:
                        if e or not first:
                            up(g, e + 1, par, 1 - b)
                    elif not final:
                        up(g + 1, 0, 1 - par, 1 - b)
                        turn_comb(g + 1)
                    if e:
                        down(g, e - 1)
                    elif not first:
                        down(g - 1, E1 - 1)
                    if not final:
                        piece(e, g + 1, 1 - par, main)

            turn_comb(0)
            group(0, 0, first=True)
            group(1, 1)
            with pe.Fori(1, G // 2 - 1) as two:
                group(two * 2, 0)
                group(two * 2 + 1, 1)
            group(G - 2, 0)
            group(G - 1, 1, final=True)
            pe.wait_ge(h_high, G * E1)
            for t in range(T4):
                for m in range(2):
                    down_product(E1 - 1, t, m)
            pe.wait_ge(h_low, G * E1)
            for t in range(T4):
                down_product(E1 - 1, t, 2).then_inc(last_down, 1)

        @block.scalar
        def _(act):
            def piece(e, g, par, sems):
                if e in (5, 6):
                    half = e - 5
                    act.wait_ge(sems["x2_turned"], (g * 2 + half + 1) * 2 * KT)
                    nc.scalar.activation(
                        x2T[:, par, 0, :, half * 2 * P:(half + 1) * 2 * P],
                        ps_misc[:, :].rearrange("p (k t) -> p k t", k=KT), ACT.Copy, scale=XS).then_inc(sems["x2_high"], 1)
                elif e == 7:
                    act.wait_ge(sems["logits_done"], (g + 1) * T4)
                    if not isinstance(g, int) or g:
                        act.wait_ge(sems["choice_step"], g * CHOICE_STEPS)
                    nc.scalar.activation(th[:, :, :], ps_misc[:, 0:T4 * E].rearrange("p (t e) -> p t e", t=T4),
                                         ACT.Tanh, scale=l_un[:, 0:1]).then_inc(sems["th_done"], 1)

            act.wait_ge(seed_clear, 1)
            nc.scalar.activation(act_warm[:, :], seed[:, 0, 0:1], ACT.Silu)

            def step(s, dst):
                act.wait_ge(scan_mm, s + 1)
                nc.scalar.activation(dst, ps_scan[s % 2][:, 0:P], ACT.Tanh).then_inc(scan_tanh, 1)

            for s in range(WARM + L):
                if s in (WARM - 1, WARM + L - 1):
                    act.wait_ge(scan_mm, s + 1)
                    nc.scalar.activation(seed[:, :, 1:NCH],
                                         ps_scan[s % 2][:, 0:P].rearrange("p (b c) -> p b c", b=NB)[:, :, 0:NCH - 1],
                                         ACT.Tanh).then_inc(scan_tanh, 1)
                else:
                    step(s, run_state[:, s % 2, :])
                if 1 <= s <= HALVES:
                    n, k = FIRST + (s - 1) // 2, (s - 1) % 2
                    act.wait_ge(xT_turned, 2 * FIRST + s)
                    nc.scalar.activation(xT[:, k, pairs[n] * 2:pairs[n] * 2 + 2, :].rearrange("p j c -> p (j c)"),
                                         ps_xT[(2 * n + k) % 4][:, 0:2 * P], ACT.Copy).then_inc(xT_done, 1)
            for i in range(L):
                step(WARM + L + i, states[:, i, :])
                if i in ACT_AT:
                    piece(ACT_AT[i], 0, 0, main)

            act.wait_ge(met_known, 1)
            runs_met = act.value_load(met[0:1, 0:1], min_val=0, max_val=1)
            with act.If(runs_met == 0):
                act.sem_inc(fb_tanh, 1)
                with act.Fori(0, NCH) as c:
                    with act.Fori(0, L // 2) as l:
                        for j in range(2):
                            act.wait_ge(fb_mm, c * L + l * 2 + (j + 1))
                            nc.scalar.activation(states[:, l * 2 + j, :].rearrange("p (b c) -> p c b", b=NB)[:, c, :],
                                                 ps_scan[j][:, 0:NB], ACT.Tanh).then_inc(fb_kept, 1)
                            nc.scalar.activation(fb_state[:, j, :], ps_scan[j][:, 0:NB], ACT.Tanh).then_inc(fb_tanh, 1)
                for e in range(E1):
                    piece(e, 0, 0, again)
                act.wait_ge(again_up, 2)

            def silu(g, e, b):
                n = g * E1 + e
                act.wait_ge(up_done, n + 1)
                if not isinstance(n, int) or n >= 2:
                    act.wait_ge(gu_done, n - 1)
                nc.scalar.activation(sg[:, b, :], ps_g[b][:, :], ACT.Silu, scale=g_un[:, 0:1]).then_inc(silu_done, 1)

            def high(g, e, b):
                n = g * E1 + e
                if e:
                    act.wait_ge(h_done, g * E + e)
                else:
                    act.wait_ge(gu_done, n + 1)
                if not isinstance(n, int) or n >= 3:
                    act.wait_ge(down_done, n - 2)
                nc.scalar.activation(h16[:, e % 3, 0, :], h[:, b, :], ACT.Copy).then_inc(h_high, 1)

            def copy_comb(g):
                act.wait_ge(comb_turned, g + 1)
                if not isinstance(g, int) or g:
                    act.wait_ge(comb_written, g * 16)
                nc.scalar.activation(combT[:, :], ps_comb[0:E, 0:GT], ACT.Copy).then_inc(combT_ready, 1)

            def group(g, par, first=False, final=False):
                for e in range(E1):
                    silu(g, e, (par + e) % 2)
                    if e == 0 and first:
                        copy_comb(0)
                    if e == 0 and not first and not final:
                        act.wait_ge(main["c_done"], (g + 1) * T4)
                        nc.scalar.activation(states16[:, 0, :, :], states[:, bass.ds((g + 1) * T4, T4), :],
                                             ACT.Copy, scale=XS).then_inc(states_high, 1)
                    if e == 7 and not final:
                        piece(e, g + 1, 1 - par, main)
                    elif e == 8 and not final:
                        copy_comb(g + 1)
                    high(g, e, (par + e) % 2)
                    if e < 7 and not final:
                        piece(e, g + 1, 1 - par, main)

            group(0, 0, first=True)
            group(1, 1)
            with act.Fori(1, G // 2 - 1) as two:
                group(two * 2, 0)
                group(two * 2 + 1, 1)
            group(G - 2, 0)
            group(G - 1, 1, final=True)

        @block.vector
        def _(dve):
            nc.vector.memset(seed[:, :, :], 0.0).then_inc(seed_clear, 1)
            nc.vector.memset(fb_state[:, :, :], 0.0).then_inc(seed_clear, 1)
            dve.wait_ge(AB_turned, 1)
            nc.vector.tensor_copy(AT[:, :], ps_mats[0][:, 0:P])
            nc.vector.tensor_copy(BT[:, :, :].rearrange("p k n -> p (k n)"), ps_mats[0][:, P:(KT + 1) * P]).then_inc(AB_done, 1)
            UN = 2.0 ** -WTOP / XS
            HS = 2.0 ** 15 / (DM * DM * 4)
            WEIGHTS = [
                (0, wg[:, :, :, :].rearrange("p e k i -> p (e k i)"), wg16[:, :, :, :, :].rearrange("p a e k i -> p a (e k i)")),
                (1, wu[:, :, :, :].rearrange("p e k i -> p (e k i)"), wu16[:, :, :, :, :].rearrange("p a e k i -> p a (e k i)")),
                (2, rwT[:, :, :].rearrange("p k e -> p (k e)"), rw16[:, :, :, :].rearrange("p a k e -> p a (k e)")),
                (3, wd[:, :, :].rearrange("p e d -> p (e d)"), wd16[:, :, :, :].rearrange("p a e d -> p a (e d)")),
                (4, CT[:, :, :].rearrange("p k d -> p (k d)"), C16[:, :, :, :].rearrange("p a k d -> p a (k d)"))]

            def greatest(i):
                nc.vector.tensor_reduce(wmax[:, i:i + 1], WEIGHTS[i][1], AX_X, ALU.max,
                                        apply_absolute_value=True).then_inc(wmax_part, 1)

            def scales():
                dve.wait_ge(wmax_known, 1)
                nc.vector.tensor_scalar(wpow[:, :], wmax_all[:, :], 2.0 ** -60, None, ALU.max).then_inc(wstep, 1)
                dve.wait_ge(wstep, 1)
                nc.vector.tensor_scalar(wpow[:, :].bitcast(I32), wpow[:, :].bitcast(I32), 0x7F800000, None,
                                        ALU.bitwise_and).then_inc(wstep, 1)
                dve.wait_ge(wstep, 2)
                nc.vector.tensor_scalar(wscale[:, :].bitcast(I32), wpow[:, :].bitcast(I32), -1.0,
                                        float((2 * 127 + WTOP) << 23), ALU.mult, ALU.add).then_inc(wstep, 1)
                nc.vector.tensor_scalar(g_un[:, :], wpow[:, 0:1], UN, None, ALU.mult).then_inc(wstep, 1)
                nc.vector.tensor_scalar(c_un[:, :], wpow[:, 4:5], UN, None, ALU.mult).then_inc(wstep, 1)
                nc.vector.tensor_scalar(l_un[:, :], wpow[:, 2:3], 0.5 * UN, None, ALU.mult).then_inc(wstep, 1)
                nc.vector.tensor_scalar(y_un[:, 1:2], wpow[:, 3:4], wpow[:, 0:1], 2.0 ** -WTOP / HS, ALU.mult, ALU.mult).then_inc(wstep, 1)
                dve.wait_ge(wstep, 7)
                nc.vector.tensor_scalar(u_un[:, 0:1], wscale[:, 0:1], 2.0 ** -WTOP * UN * HS, None, ALU.mult).then_inc(wstep, 1)
                nc.vector.tensor_scalar(y_un[:, 0:1], y_un[:, 1:2], wpow[:, 1:2], None, ALU.mult).then_inc(wstep, 1)
                dve.wait_ge(wstep, 9)

            def split(i):
                _, flat, parts = WEIGHTS[i]
                nc.vector.tensor_scalar(parts[:, 0, :], flat, wscale[:, i:i + 1], None, ALU.mult).then_inc(w_high[i], 1)
                dve.wait_ge(w_high[i], 1)
                nc.vector.scalar_tensor_tensor(parts[:, 1, :], flat, wscale[:, i:i + 1], parts[:, 0, :],
                                               ALU.mult, ALU.subtract).then_inc(weights_ready, 1)

            for n in range(FIRST):
                for k in range(KT):
                    dve.wait_ge(xT_turned, 2 * n + k + 1)
                    nc.vector.tensor_copy(xT[:, k, pairs[n] * 2:pairs[n] * 2 + 2, :].rearrange("p j c -> p (j c)"),
                                          ps_xT[2 * n + k][:, 0:2 * P]).then_inc(xT_first, 1)
            dve.wait_ge(Cr_turned, 1)
            nc.vector.tensor_copy(rwT[:, :, :].rearrange("p k n -> p (k n)"),
                                  ps_mats[1][:, KT * P:KT * P + KT * E]).then_inc(Cr_done, 1)
            nc.vector.tensor_copy(CT[:, :, :].rearrange("p k n -> p (k n)"),
                                  ps_mats[1][:, 0:KT * P]).then_inc(Cr_done, 1)
            dve.wait_ge(Cr_done, 2)
            greatest(2)
            greatest(4)
            for i in (0, 1, 3):
                dve.wait_ge(w_in[min(i, 2)], 16 * 2)
                greatest(i)
            scales()
            for i in (0, 1, 3, 2):
                split(i)

            def stats(k, g, src, st_sem, mv_sem, t0, t1):
                for t in range(t0, t1):
                    nc.vector.bn_stats(st[:, k, t, :], src(t)).then_inc(st_sem, 1)
                dve.wait_ge(st_sem, g * T4 + t1)
                nc.vector.memset(carrier[:, :], 0.0)
                for t in range(t0, t1):
                    nc.vector.bn_aggr(mv[:, k, t, :], st[:, k, t, :]).then_inc(mv_sem, 1)

            def piece(e, g, par, sems):
                if e in (1, 2):
                    e -= 1
                    dve.wait_ge(sems["c_done"], g * T4 + 2 * (e + 1))
                    dst, sums = y1[:, 2 * e:2 * e + 2, :], ps_misc[:, :].rearrange("p (j d) -> p j d", j=2)
                    skip = xskip[:, bass.ds(g * T4 + 2 * e, 2), :]
                    if isinstance(g, int) and g < WHOLE:
                        nc.vector.tensor_tensor(dst, sums, skip, ALU.add).then_inc(sems["y1_done"], 1)
                    else:
                        nc.vector.scalar_tensor_tensor(dst, sums, c_un[:, 0:1], skip, ALU.mult, ALU.add
                                                       ).then_inc(sems["y1_done"], 1)
                    dve.wait_ge(sems["y1_done"], g * 2 + (e + 1))
                    stats(0, g, lambda t: y1[:, t, :], sems["st1_done"], sems["mv1_done"], 2 * e, 2 * e + 2)
                    dve.wait_ge(sems["mv1_done"], g * T4 + 2 * (e + 1))
                    for t in (2 * e, 2 * e + 1):
                        nc.vector.scalar_tensor_tensor(y1[:, t, :], y1[:, t, :], mv[:, 0, t, 0:1], gamma_bc[:, :],
                                                       ALU.subtract, ALU.mult).then_inc(sems["scaled1"], 1)
                elif e == 3:
                    dve.wait_ge(sems["rstd1_ready"], g + 1)
                    for t in range(T4):
                        dve.wait_ge(sems["scaled1"], g * T4 + (t + 1))
                        nc.vector.scalar_tensor_tensor(y1[:, t, :], y1[:, t, :], rstd[:, 0, 1, t:t + 1],
                                                       xres[:, g * T4 + t, :], ALU.mult, ALU.add).then_inc(sems["z1_done"], 1)
                    dve.wait_ge(sems["z1_done"], (g + 1) * T4)
                    stats(1, g, lambda t: y1[:, t, :], sems["st2_done"], sems["mv2_done"], 0, T4)
                elif e == 4:
                    dve.wait_ge(sems["rstd2_ready"], g + 1)
                    dve.wait_ge(sems["mv2_done"], (g + 1) * T4)
                    for t in range(T4):
                        nc.vector.tensor_scalar(x2[:, par, t, :], y1[:, t, :], mv[:, 1, t, 0:1],
                                                rstd[:, 1, 1, t:t + 1], ALU.subtract, ALU.mult).then_inc(sems["x2_ready"], 1)
                elif e in (5, 6):
                    half = e - 5
                    dve.wait_ge(sems["x2_high"], g * 2 + half + 1)
                    nc.vector.scalar_tensor_tensor(
                        x2T[:, par, 1, :, half * 2 * P:(half + 1) * 2 * P],
                        ps_misc[:, :].rearrange("p (k t) -> p k t", k=KT), XS,
                        x2T[:, par, 0, :, half * 2 * P:(half + 1) * 2 * P], ALU.mult, ALU.subtract).then_inc(sems["x2_low"], 1)

            tt, ts = nc.vector.tensor_tensor, nc.vector.tensor_scalar

            def choose(g, sems):
                done = 0

                def then(ins):
                    nonlocal done
                    done += 1
                    ins.then_inc(sems["choice_step"], 1)
                    dve.wait_ge(sems["choice_step"], g * CHOICE_STEPS + done)

                dve.wait_ge(sems["th_done"], g + 1)
                then(ts(score[:, :, :], th[:, :, :], 0.5, 0.5, ALU.mult, ALU.add))
                then(tt(choice[:, :, :], score[:, :, :], cbias_bc[:, :].unsqueeze(1).to_broadcast([P, T4, E]), ALU.add))
                by2 = choice[:, :, :].rearrange("p t (q a) -> p t q a", a=2)
                tt(more[:, :, :], by2[:, :, :, 0], by2[:, :, :, 1], ALU.max)
                then(tt(both[:, :, :], by2[:, :, :, 0], by2[:, :, :, 1], ALU.add))
                more2 = more[:, :, :].rearrange("p t (q a) -> p t q a", a=2)
                both2 = both[:, :, :].rearrange("p t (q a) -> p t q a", a=2)
                tt(top[:, :, :], both2[:, :, :, 0], both2[:, :, :, 1], ALU.max)
                then(tt(across[:, :, :], more2[:, :, :, 0], more2[:, :, :, 1], ALU.add))
                then(tt(top[:, :, :], top[:, :, :], across[:, :, :], ALU.max))
                tt(mask[:, :, 0:1], top[:, :, 0:1], top[:, :, 1:2], ALU.is_ge)
                then(tt(mask[:, :, 1:2], top[:, :, 0:1], top[:, :, 1:2], ALU.is_lt))
                by_group = choice[:, :, :].rearrange("p t (q a) -> p t q a", q=2)
                then(tt(by_group, by_group, mask[:, :, :].unsqueeze(3).to_broadcast([P, T4, 2, EPG]), ALU.mult))
                of_j = choice[:, :, :].unsqueeze(2).to_broadcast([P, T4, E, E])
                of_i = choice[:, :, :].unsqueeze(3).to_broadcast([P, T4, E, E])
                tt(ahead[:, :, :, :], of_j, of_i, ALU.is_gt)
                then(tt(level[:, :, :, :], of_j, of_i, ALU.is_equal))
                then(tt(level[:, :, :, :], level[:, :, :, :], lower[:, :, :].unsqueeze(1).to_broadcast([P, T4, E, E]), ALU.mult))
                then(tt(ahead[:, :, :, :], ahead[:, :, :, :], level[:, :, :, :], ALU.add))
                assert done == CHOICE_STEPS, done

            def weigh(g, sems):
                done = 0

                def then(ins):
                    nonlocal done
                    done += 1
                    ins.then_inc(sems["route_step"], 1)
                    dve.wait_ge(sems["route_step"], g * STEPS + done)

                then(nc.vector.tensor_reduce(rank[:, :, :], ahead[:, :, :, :], AX_X, ALU.add))
                flat = [v[:, :, :].rearrange("p t e -> p (t e)") for v in (kept, rank, score)]
                then(nc.vector.scalar_tensor_tensor(flat[0], flat[1], 2.0, flat[2], ALU.is_lt, ALU.mult))
                then(nc.vector.tensor_reduce(total[:, :, 0], kept[:, :, :], AX_X, ALU.add))
                then(ts(total[:, :, 1], total[:, :, 0], 1e-20, None, ALU.add))
                then(nc.vector.reciprocal(total[:, :, 0], total[:, :, 1]))
                if not isinstance(g, int) or g:
                    dve.wait_ge(comb_turned, g)
                then(tt(comb[:, :, :], kept[:, :, :], total[:, :, 0:1].to_broadcast([P, T4, E]), ALU.mult))
                assert done == STEPS, done

            dve.wait_ge(res_done, 2)
            dve.wait_ge(weights_ready, 4)
            for e in range(E1):
                piece(e, 0, 0, main)
                if e == 4:
                    split(4)
            choose(0, main)
            weigh(0, main)

            dve.wait_ge(scan_tanh, WARM + 2 * L)
            nc.vector.tensor_tensor(met_diff[:, :, :],
                                    states[:, L - 1, :].rearrange("p (b c) -> p b c", b=NB)[:, :, 0:NCH - 1],
                                    seed[:, :, 1:NCH], ALU.subtract).then_inc(met_step, 1)
            dve.wait_ge(met_step, 1)
            nc.vector.tensor_reduce(met_row[:, 0:1], met_diff[:, :, :].rearrange("p b c -> p (b c)"), AX_X, ALU.max,
                                    apply_absolute_value=True).then_inc(met_part, 1)
            dve.wait_ge(met_all, 1)
            nc.vector.tensor_scalar(met[:, :], met_row[:, 1:2], MET, None, ALU.is_le).then_inc(met_known, 1)
            dve.wait_ge(met_known, 1)
            runs_met = dve.value_load(met[0:1, 0:1], min_val=0, max_val=1)
            with dve.If(runs_met == 0):
                for e in range(E1):
                    piece(e, 0, 0, again)
                choose(0, again)
                weigh(0, again)

            def inner(g, e, b):
                n = g * E1 + e
                dve.wait_ge(silu_done, n + 1)
                if not isinstance(n, int) or n >= 2:
                    dve.wait_ge(h_low, n - 1)
                if e == 0:
                    nc.vector.scalar_tensor_tensor(h[:, b, :], ps_u[b][:, :], u_un[:, 0:1], sg[:, b, :],
                                                   ALU.mult, ALU.mult).then_inc(gu_done, 1)
                else:
                    nc.vector.scalar_tensor_tensor(gu[:, b, :], ps_u[b][:, :], u_un[:, 0:1], sg[:, b, :],
                                                   ALU.mult, ALU.mult).then_inc(gu_done, 1)
                    dve.wait_ge(gu_done, n + 1)
                    dve.wait_ge(comb_in[e - 1], (g + 1) * 16)
                    nc.vector.tensor_tensor(h[:, b, :], comb_all[:, e - 1, :], gu[:, b, :], ALU.mult).then_inc(h_done, 1)

            def close(step, g, par):
                if step == 0:
                    dve.wait_ge(down_done, (g + 1) * E1)
                    for j in range(2):
                        part = x2[:, par, 2 * j:2 * j + 2, :]
                        nc.vector.scalar_tensor_tensor(z2[:, 2 * j:2 * j + 2, :], ps_y[j][:, :].rearrange("p (j d) -> p j d", j=2),
                                                       y_un[:, 0:1], part, ALU.mult, ALU.add).then_inc(z2_done, 1)
                elif step == 1:
                    dve.wait_ge(z2_done, (g + 1) * 2)
                    stats(2, g, lambda t: z2[:, t, :], st3_done, mv3_done, 0, T4)
                else:
                    dve.wait_ge(rstd3_ready, g + 1)
                    dve.wait_ge(mv3_done, (g + 1) * T4)
                    for t in range(T4):
                        nc.vector.tensor_scalar(xskip[:, g * T4 + t, :], z2[:, t, :], mv[:, 2, t, 0:1],
                                                rstd[:, 2, 1, t:t + 1], ALU.subtract, ALU.mult).then_inc(out_ready, 1)

            def group(g, par, first=False, final=False):
                for e in range(E1):
                    if e == 1 and first:
                        piece(1, 1, 1, main)
                    inner(g, e, (par + e) % 2)
                    if e == 0 and not first and not final:
                        dve.wait_ge(states_high, g + 2 - WHOLE)
                        nc.vector.scalar_tensor_tensor(states16[:, 1, :, :], states[:, bass.ds((g + 1) * T4, T4), :], XS,
                                                       states16[:, 0, :, :], ALU.mult, ALU.subtract).then_inc(states_low, 1)
                    if e in (1, 5, 6) and not first:
                        close((1, 5, 6).index(e), g - 1, 1 - par)
                    if not final:
                        if e > 1 or not first:
                            piece(e, g + 1, 1 - par, main)
                        if e == 7:
                            choose(g + 1, main)
                            weigh(g + 1, main)

            dve.wait_ge(res_done, L // T4)
            group(0, 0, first=True)
            group(1, 1)
            with dve.Fori(1, G // 2 - 1) as two:
                group(two * 2, 0)
                group(two * 2 + 1, 1)
            group(G - 2, 0)
            group(G - 1, 1, final=True)
            g = G - 1
            for half in range(2):
                dve.wait_ge(last_down, 2 * (half + 1))
                part = x2[:, g % 2, 2 * half:2 * half + 2, :]
                nc.vector.scalar_tensor_tensor(z2[:, 2 * half:2 * half + 2, :], ps_y[half][:, :].rearrange("p (j d) -> p j d", j=2),
                                               y_un[:, 0:1], part, ALU.mult, ALU.add).then_inc(z2_done, 1)
                dve.wait_ge(z2_done, g * 2 + half + 1)
                stats(2, g, lambda t: z2[:, t, :], st3_done, mv3_done, 2 * half, 2 * half + 2)
            for half in range(2):
                dve.wait_ge(rstd3_ready, g + half + 1)
                for t in (2 * half, 2 * half + 1):
                    nc.vector.tensor_scalar(xskip[:, g * T4 + t, :], z2[:, t, :], mv[:, 2, t, 0:1],
                                            rstd[:, 2, 1, t:t + 1], ALU.subtract, ALU.mult).then_inc(out_ready, 1)

        @block.gpsimd
        def _(pool):
            nc.gpsimd.memset(ident[:, :], 0.0).then_inc(const_step, 1)
            pool.wait_ge(const_step, 1)
            nc.gpsimd.affine_select(out=ident[:, :], in_=ident[:, :], compare_op=ALU.not_equal, fill=1.0, base=0,
                                    pattern=[[-1, P]], channel_multiplier=1).then_inc(consts, 1)
            nc.gpsimd.memset(lower[:, :, :], 1.0).then_inc(const_step, 1)
            pool.wait_ge(const_step, 2)
            nc.gpsimd.affine_select(out=lower[:, :, :], in_=lower[:, :, :], compare_op=ALU.is_gt, fill=0.0, base=0,
                                    pattern=[[1, E], [-1, E]], channel_multiplier=0)
            nc.gpsimd.memset(eps[:, :], LN_EPS)
            nc.gpsimd.memset(neghalf[:, :], -0.5).then_inc(const_step, 1)
            pool.wait_ge(const_step, 3)
            pool.wait_ge(D_in, 16)
            nc.gpsimd.tensor_scalar(D_bc[:, :], D_bc[:, :], 1.0, None, ALU.add).then_inc(const_step, 1)
            pool.wait_ge(const_step, 4)

            def skip(n):
                c = chunks[n]
                pool.wait_ge(x_in[c], 16)
                if n == 0:
                    pool.wait_ge(x_rest, 16)
                nc.gpsimd.tensor_tensor(xskip[:, c * T4:(c + 1) * T4, :], xres[:, c * T4:(c + 1) * T4, :],
                                        D_bc[:, :].unsqueeze(1).to_broadcast([P, T4, DM]), ALU.mult).then_inc(skip_done, 1)

            def residual(n):
                c = chunks[n]
                pool.wait_ge(skip_done, n + 1)
                pool.wait_ge(xT_turned, T4 * (n + 1))
                nc.gpsimd.tensor_tensor(xres[:, c * T4:(c + 1) * T4, :], xres[:, c * T4:(c + 1) * T4, :],
                                        beta_bc[:, :].unsqueeze(1).to_broadcast([P, T4, DM]), ALU.add).then_inc(res_done, 1)

            for n in range(L // T4):
                skip(n)
                if n == 6:
                    pool.wait_ge(wmax_part, 5)
                    nc.gpsimd.partition_all_reduce(wmax_all[:, :], wmax[:, :], P, RMAX).then_inc(wmax_known, 1)
            pool.wait_ge(vecs_in, 16 * NVEC)
            for n in range(L // T4 - 2):
                residual(n)

            def rsqrt(k, g, mv_sem, step_sem, ready, count, t0=0, t1=T4):
                pool.wait_ge(mv_sem, g * T4 + t1)
                nc.gpsimd.tensor_tensor(rstd[:, k, 0, t0:t1], mv[:, k, t0:t1, 1], eps[:, t0:t1], ALU.add).then_inc(step_sem, 1)
                pool.wait_ge(step_sem, count + 1)
                nc.gpsimd.tensor_tensor(rstd[:, k, 1, t0:t1], rstd[:, k, 0, t0:t1], neghalf[:, t0:t1], ALU.pow).then_inc(ready, 1)

            rsqrt(0, 0, main["mv1_done"], rstd_step, main["rstd1_ready"], 0)
            residual(L // T4 - 2)
            rsqrt(1, 0, main["mv2_done"], rstd_step, main["rstd2_ready"], 1)
            residual(L // T4 - 1)
            pool.wait_ge(met_part, 1)
            nc.gpsimd.partition_all_reduce(met_row[:, 1:2], met_row[:, 0:1], P, RMAX).then_inc(met_all, 1)
            pool.wait_ge(met_known, 1)
            runs_met = pool.value_load(met[0:1, 0:1], min_val=0, max_val=1)
            with pool.If(runs_met == 0):
                rsqrt(0, 0, again["mv1_done"], again_rstd_step, again["rstd1_ready"], 0)
                rsqrt(1, 0, again["mv2_done"], again_rstd_step, again["rstd2_ready"], 1)

            def low(g, e, b):
                pool.wait_ge(h_high, g * E1 + (e + 1))
                nc.gpsimd.tensor_tensor(h16[:, e % 3, 1, :], h[:, b, :], h16[:, e % 3, 0, :], ALU.subtract).then_inc(h_low, 1)

            def group(g, par, first=False, final=False):
                count = g * 3 + (2 if first else 1)
                for e in range(E1):
                    low(g, e, (par + e) % 2)
                    if e == 2 and not final:
                        rsqrt(0, g + 1, main["mv1_done"], rstd_step, main["rstd1_ready"], count)
                    elif e == 3 and not final:
                        rsqrt(1, g + 1, main["mv2_done"], rstd_step, main["rstd2_ready"], count + 1)
                    elif e == 5 and not first:
                        rsqrt(2, g - 1, mv3_done, rstd_step, rstd3_ready, count + (0 if final else 2))

            group(0, 0, first=True)
            group(1, 1)
            with pool.Fori(1, G // 2 - 1) as two:
                group(two * 2, 0)
                group(two * 2 + 1, 1)
            group(G - 2, 0)
            group(G - 1, 1, final=True)
            for half in range(2):
                rsqrt(2, G - 1, mv3_done, rstd_step, rstd3_ready, (G - 1) * 3 + 2 + half, 2 * half, 2 * half + 2)


_INS = ["L0_attn_x", "L0_attn_A", "L0_attn_B", "L0_attn_C", "L0_attn_D", "L0_attn_gamma", "L0_attn_beta",
        "L0_ffn_router_weight", "L0_ffn_correction_bias", "L0_ffn_w_gate", "L0_ffn_w_up", "L0_ffn_w_down",
        "L0_ffn_sw_gate", "L0_ffn_sw_up", "L0_ffn_sw_down"]


def kernel(**inputs):
    import numpy as np
    import concourse.bacc as bacc
    from concourse.bass_utils import run_bass_kernel_spmd

    nc = bacc.Bacc("TRN2", target_bir_lowering=False, num_devices=1)
    arrays, args = {}, []
    for name in _INS:
        a = np.ascontiguousarray(inputs[name])
        arrays[f"in_{name}_dram"] = a
        args.append(nc.dram_tensor(f"in_{name}_dram", a.shape, mybir.dt.from_np(a.dtype), kind="ExternalInput").ap())
    shape = inputs["L0_attn_x"].shape
    args.append(nc.dram_tensor("comb_dram", (*inputs["L0_ffn_router_weight"].shape[:1], shape[0] * shape[1]), F32,
                               kind="Internal").ap())
    args.append(nc.dram_tensor("out_0_dram", shape, F32, kind="ExternalOutput").ap())
    ssm_moe_kernel(nc, *args)
    r = run_bass_kernel_spmd(nc, [arrays], core_ids=[0])
    return r.results[0]["out_0_dram"]
```
